# Optimizing a Trainium2 kernel written in Bass

```python
import numpy as np
import jax
import jax.numpy as jnp

def _softmax(x, axis=-1):
    return jax.nn.softmax(x, axis=axis)

def _gelu(x):
    return jax.nn.gelu(x, approximate=True)

def _silu(x):
    return jax.nn.silu(x)

def _sigmoid(x):
    return jax.nn.sigmoid(x)

def _layernorm(x, axis=-1, eps=1e-05):
    m = jnp.mean(x, axis=axis, keepdims=True)
    v = jnp.var(x, axis=axis, keepdims=True)
    return (x - m) / jnp.sqrt(v + eps)

def _scatter_add(tgt, idx, src, axis=0):
    return tgt.at[idx].add(src)

def _segment_sum(src, seg, n):
    return jax.ops.segment_sum(src, seg, n)
kernel_name = 'mk_adaln_d1_jaxref_r8_4c14a4'

def setup_inputs(seed: int=0):
    np.random.seed(seed)
    _w = jnp.asarray

    def _L0_attn_setup():
        import jax, jax.numpy as jnp
        import numpy as np
        B, S, D = (2, 256, 128)
        H, DH = (16, 64)
        DQL, DKVL = (64, 64)
        DR = 64
        TOPK = 64
        LN_EPS = 1e-05
        ROPE_BASE = 10000.0

        def _rope_tables(seq_len, dim):
            inv_freq = 1.0 / ROPE_BASE ** (np.arange(0, dim, 2, dtype=np.float32) / dim)
            t = np.arange(seq_len, dtype=np.float32)
            freqs = np.outer(t, inv_freq)
            cos = np.concatenate([np.cos(freqs), np.cos(freqs)], -1)[:, ::2]
            sin = np.concatenate([np.sin(freqs), np.sin(freqs)], -1)[:, ::2]
            return (jnp.asarray(cos), jnp.asarray(sin))

        def _apply_rope_subspace(x, d_rope):
            s = x.shape[-2]
            cos, sin = _rope_tables(s, d_rope)
            xr, xp = (x[..., :d_rope], x[..., d_rope:])
            e, o = (xr[..., 0::2], xr[..., 1::2])
            rot = jnp.stack([e * cos - o * sin, e * sin + o * cos], axis=-1).reshape(xr.shape)
            return jnp.concatenate([rot, xp], axis=-1)

        def _reference_tuple_inner(x, w_down_q, w_down_kv, w_up_q, w_up_k, w_up_v, w_out, ln_scale, ln_bias):
            b, s, d = x.shape
            residual = x
            mu = jnp.mean(x, axis=-1, keepdims=True)
            var = jnp.mean((x - mu) ** 2, axis=-1, keepdims=True)
            h = (x - mu) * jax.lax.rsqrt(var + LN_EPS) * ln_scale + ln_bias
            c_q = h @ w_down_q.T
            c_kv = h @ w_down_kv.T
            q = (c_q @ w_up_q.T).reshape(b, s, H, DH).transpose(0, 2, 1, 3)
            k = (c_kv @ w_up_k.T).reshape(b, s, H, DH).transpose(0, 2, 1, 3)
            v = (c_kv @ w_up_v.T).reshape(b, s, H, DH).transpose(0, 2, 1, 3)
            q = _apply_rope_subspace(q, DR)
            k = _apply_rope_subspace(k, DR)
            scale = 1.0 / np.sqrt(DH).astype(np.float32)
            scores = jnp.einsum('bhqd,bhkd->bhqk', q, k) * scale
            _, indices = jax.lax.top_k(scores, min(TOPK, s))
            attn = jax.nn.softmax(scores, axis=-1)
            out = jnp.einsum('bhqk,bhkd->bhqd', attn, v)
            out = out.transpose(0, 2, 1, 3).reshape(b, s, H * DH)
            out = out @ w_out.T + residual
            return (out, indices.astype(jnp.int64))
        key = jax.random.key(seed)
        ks = jax.random.split(key, 7)
        init = lambda k, shape: jax.random.normal(k, shape, jnp.float32) * 0.02
        return {'x': jax.random.normal(ks[0], (B, S, D), jnp.float32), 'w_down_q': init(ks[1], (DQL, D)), 'w_down_kv': init(ks[2], (DKVL, D)), 'w_up_q': init(ks[3], (H * DH, DQL)), 'w_up_k': init(ks[4], (H * DH, DKVL)), 'w_up_v': init(ks[5], (H * DH, DKVL)), 'w_out': init(ks[6], (D, H * DH)), 'ln_scale': jnp.ones((D,), jnp.float32), 'ln_bias': jnp.zeros((D,), jnp.float32)}
    _L0_attn_in = _L0_attn_setup()

    def _L0_ffn_setup():
        import jax, jax.numpy as jnp
        import numpy as np
        from jax import lax
        HIDDEN = 128
        INTER = 64
        E = 64
        K = 6
        G = 8
        TG = 4
        NSH = 2
        ISH = INTER * NSH

        def _moe_forward(hidden_states, gate_w, gate_bias, eg_w, eu_w, ed_w, sg_w, su_w, sd_w):
            B, S, H = hidden_states.shape
            x = hidden_states.reshape(-1, H)
            T = x.shape[0]
            shared = jax.nn.silu(x @ sg_w.T) * (x @ su_w.T) @ sd_w.T
            logits = x @ gate_w.T
            scores = jax.nn.sigmoid(logits) + gate_bias
            group_scores = scores.reshape(T, G, E // G).max(axis=-1)
            _, sel_groups = lax.top_k(group_scores, TG)
            group_mask = jnp.zeros((T, G), scores.dtype).at[jnp.arange(T)[:, None], sel_groups].set(1.0)
            mask = jnp.repeat(group_mask, E // G, axis=1)
            masked_scores = scores * mask
            topk_w, topk_i = lax.top_k(masked_scores, K)
            topk_w = topk_w / (topk_w.sum(axis=-1, keepdims=True) + 1e-08)
            comb = jnp.zeros((T, E), x.dtype).at[jnp.arange(T)[:, None], topk_i].add(topk_w)
            h = jax.nn.silu(jnp.einsum('th,eih->eti', x, eg_w)) * jnp.einsum('th,eih->eti', x, eu_w)
            routed = jnp.einsum('eti,ehi,te->th', h, ed_w, comb)
            return (shared + routed).reshape(B, S, H)
        key = jax.random.key(seed)
        ks = jax.random.split(key, 9)
        s = 0.02
        return {'hidden_states': jax.random.normal(ks[0], (1, 128, HIDDEN), jnp.float32), 'gate_w': jax.random.normal(ks[1], (E, HIDDEN), jnp.float32) * s, 'gate_bias': jnp.zeros((E,), jnp.float32), 'eg_w': jax.random.normal(ks[2], (E, INTER, HIDDEN), jnp.float32) * s, 'eu_w': jax.random.normal(ks[3], (E, INTER, HIDDEN), jnp.float32) * s, 'ed_w': jax.random.normal(ks[4], (E, HIDDEN, INTER), jnp.float32) * s, 'sg_w': jax.random.normal(ks[5], (ISH, HIDDEN), jnp.float32) * s, 'su_w': jax.random.normal(ks[6], (ISH, HIDDEN), jnp.float32) * s, 'sd_w': jax.random.normal(ks[7], (HIDDEN, ISH), jnp.float32) * s}
    _L0_ffn_in = _L0_ffn_setup()
    _L0_c = _w((lambda *s: np.random.randn(*s).astype(np.float32) * 0.05)(8, 128))
    _L0_wmod = _w((lambda *s: np.random.randn(*s).astype(np.float32) * 0.05)(128, 6 * 128) * 128 ** (-0.5))
    _d = {'L0_attn_x': _L0_attn_in['x'], 'L0_attn_w_down_q': _L0_attn_in['w_down_q'], 'L0_attn_w_down_kv': _L0_attn_in['w_down_kv'], 'L0_attn_w_up_q': _L0_attn_in['w_up_q'], 'L0_attn_w_up_k': _L0_attn_in['w_up_k'], 'L0_attn_w_up_v': _L0_attn_in['w_up_v'], 'L0_attn_w_out': _L0_attn_in['w_out'], 'L0_attn_ln_scale': _L0_attn_in['ln_scale'], 'L0_attn_ln_bias': _L0_attn_in['ln_bias'], 'L0_ffn_gate_w': _L0_ffn_in['gate_w'], 'L0_ffn_gate_bias': _L0_ffn_in['gate_bias'], 'L0_ffn_eg_w': _L0_ffn_in['eg_w'], 'L0_ffn_eu_w': _L0_ffn_in['eu_w'], 'L0_ffn_ed_w': _L0_ffn_in['ed_w'], 'L0_ffn_sg_w': _L0_ffn_in['sg_w'], 'L0_ffn_su_w': _L0_ffn_in['su_w'], 'L0_ffn_sd_w': _L0_ffn_in['sd_w'], 'L0_c': _L0_c, 'L0_wmod': _L0_wmod}
    _x0 = _d['L0_attn_x']
    _d['L0_attn_x'] = jax.random.normal(jax.random.fold_in(jax.random.key(seed), 1), (8, 256, 128), dtype=_x0.dtype)
    del _x0
    return _d

def reference(L0_attn_x, L0_attn_w_down_q, L0_attn_w_down_kv, L0_attn_w_up_q, L0_attn_w_up_k, L0_attn_w_up_v, L0_attn_w_out, L0_attn_ln_scale, L0_attn_ln_bias, L0_ffn_gate_w, L0_ffn_gate_bias, L0_ffn_eg_w, L0_ffn_eu_w, L0_ffn_ed_w, L0_ffn_sg_w, L0_ffn_su_w, L0_ffn_sd_w, L0_c, L0_wmod):

    def _L0_attn_ref(x, w_down_q, w_down_kv, w_up_q, w_up_k, w_up_v, w_out, ln_scale, ln_bias):
        import jax, jax.numpy as jnp
        import numpy as np
        B, S, D = (2, 256, 128)
        H, DH = (16, 64)
        DQL, DKVL = (64, 64)
        DR = 64
        TOPK = 64
        LN_EPS = 1e-05
        ROPE_BASE = 10000.0

        def _rope_tables(seq_len, dim):
            inv_freq = 1.0 / ROPE_BASE ** (np.arange(0, dim, 2, dtype=np.float32) / dim)
            t = np.arange(seq_len, dtype=np.float32)
            freqs = np.outer(t, inv_freq)
            cos = np.concatenate([np.cos(freqs), np.cos(freqs)], -1)[:, ::2]
            sin = np.concatenate([np.sin(freqs), np.sin(freqs)], -1)[:, ::2]
            return (jnp.asarray(cos), jnp.asarray(sin))

        def _apply_rope_subspace(x, d_rope):
            s = x.shape[-2]
            cos, sin = _rope_tables(s, d_rope)
            xr, xp = (x[..., :d_rope], x[..., d_rope:])
            e, o = (xr[..., 0::2], xr[..., 1::2])
            rot = jnp.stack([e * cos - o * sin, e * sin + o * cos], axis=-1).reshape(xr.shape)
            return jnp.concatenate([rot, xp], axis=-1)

        def _reference_tuple_inner(x, w_down_q, w_down_kv, w_up_q, w_up_k, w_up_v, w_out, ln_scale, ln_bias):
            b, s, d = x.shape
            residual = x
            mu = jnp.mean(x, axis=-1, keepdims=True)
            var = jnp.mean((x - mu) ** 2, axis=-1, keepdims=True)
            h = (x - mu) * jax.lax.rsqrt(var + LN_EPS) * ln_scale + ln_bias
            c_q = h @ w_down_q.T
            c_kv = h @ w_down_kv.T
            q = (c_q @ w_up_q.T).reshape(b, s, H, DH).transpose(0, 2, 1, 3)
            k = (c_kv @ w_up_k.T).reshape(b, s, H, DH).transpose(0, 2, 1, 3)
            v = (c_kv @ w_up_v.T).reshape(b, s, H, DH).transpose(0, 2, 1, 3)
            q = _apply_rope_subspace(q, DR)
            k = _apply_rope_subspace(k, DR)
            scale = 1.0 / np.sqrt(DH).astype(np.float32)
            scores = jnp.einsum('bhqd,bhkd->bhqk', q, k) * scale
            _, indices = jax.lax.top_k(scores, min(TOPK, s))
            attn = jax.nn.softmax(scores, axis=-1)
            out = jnp.einsum('bhqk,bhkd->bhqd', attn, v)
            out = out.transpose(0, 2, 1, 3).reshape(b, s, H * DH)
            out = out @ w_out.T + residual
            return (out, indices.astype(jnp.int64))
        return _reference_tuple_inner(x, w_down_q, w_down_kv, w_up_q, w_up_k, w_up_v, w_out, ln_scale, ln_bias)[0]

    def _L0_ffn_ref(hidden_states, gate_w, gate_bias, eg_w, eu_w, ed_w, sg_w, su_w, sd_w):
        import jax, jax.numpy as jnp
        import numpy as np
        from jax import lax
        HIDDEN = 128
        INTER = 64
        E = 64
        K = 6
        G = 8
        TG = 4
        NSH = 2
        ISH = INTER * NSH

        def _moe_forward(hidden_states, gate_w, gate_bias, eg_w, eu_w, ed_w, sg_w, su_w, sd_w):
            B, S, H = hidden_states.shape
            x = hidden_states.reshape(-1, H)
            T = x.shape[0]
            shared = jax.nn.silu(x @ sg_w.T) * (x @ su_w.T) @ sd_w.T
            logits = x @ gate_w.T
            scores = jax.nn.sigmoid(logits) + gate_bias
            group_scores = scores.reshape(T, G, E // G).max(axis=-1)
            _, sel_groups = lax.top_k(group_scores, TG)
            group_mask = jnp.zeros((T, G), scores.dtype).at[jnp.arange(T)[:, None], sel_groups].set(1.0)
            mask = jnp.repeat(group_mask, E // G, axis=1)
            masked_scores = scores * mask
            topk_w, topk_i = lax.top_k(masked_scores, K)
            topk_w = topk_w / (topk_w.sum(axis=-1, keepdims=True) + 1e-08)
            comb = jnp.zeros((T, E), x.dtype).at[jnp.arange(T)[:, None], topk_i].add(topk_w)
            h = jax.nn.silu(jnp.einsum('th,eih->eti', x, eg_w)) * jnp.einsum('th,eih->eti', x, eu_w)
            routed = jnp.einsum('eti,ehi,te->th', h, ed_w, comb)
            return (shared + routed).reshape(B, S, H)
        return _moe_forward(hidden_states, gate_w, gate_bias, eg_w, eu_w, ed_w, sg_w, su_w, sd_w)
    x = L0_attn_x
    mod = (_silu(L0_c) @ L0_wmod).reshape(L0_c.shape[0], 6, 1, -1)
    sa, ca, ga, sb, cb, gb = (mod[:, 0], mod[:, 1], mod[:, 2], mod[:, 3], mod[:, 4], mod[:, 5])
    ga = (2 * (ga >= 0) - 1) * jnp.maximum(jnp.abs(ga), 0.25)
    gb = (2 * (gb >= 0) - 1) * jnp.maximum(jnp.abs(gb), 0.25)
    h = _layernorm(x, axis=-1) * (1 + ca) + sa
    x = x + ga * _L0_attn_ref(h, L0_attn_w_down_q, L0_attn_w_down_kv, L0_attn_w_up_q, L0_attn_w_up_k, L0_attn_w_up_v, L0_attn_w_out, L0_attn_ln_scale, L0_attn_ln_bias)
    h = _layernorm(x, axis=-1) * (1 + cb) + sb
    x = x + gb * _L0_ffn_ref(h, L0_ffn_gate_w, L0_ffn_gate_bias, L0_ffn_eg_w, L0_ffn_eu_w, L0_ffn_ed_w, L0_ffn_sg_w, L0_ffn_su_w, L0_ffn_sd_w)
    return x

_drawn_inputs = setup_inputs


def setup_inputs(seed=0):
    import zlib

    import numpy as np

    out = dict(_drawn_inputs(seed))
    spreads = {'L0_attn_ln_scale': (1.0, 0.6),
     'L0_attn_ln_bias': (0.0, 0.8),
     'L0_ffn_gate_bias': (0.0, 0.8)}
    factors = {'L0_attn_w_down_q': 8.0,
     'L0_attn_w_down_kv': 8.0,
     'L0_attn_w_up_q': 8.0,
     'L0_attn_w_up_k': 8.0,
     'L0_attn_w_up_v': 8.0,
     'L0_attn_w_out': 8.0,
     'L0_ffn_gate_w': 8.0,
     'L0_ffn_eg_w': 8.0,
     'L0_ffn_eu_w': 8.0,
     'L0_ffn_ed_w': 8.0,
     'L0_ffn_sg_w': 8.0,
     'L0_ffn_su_w': 8.0,
     'L0_ffn_sd_w': 8.0}
    for name, (base, spread) in spreads.items():
        noise = np.random.default_rng([zlib.crc32(name.encode()), seed]).standard_normal(out[name].shape)
        drawn = base * np.exp(spread * noise) if base else spread * noise
        out[name] = jnp.asarray(drawn.astype(out[name].dtype))
    for name, factor in factors.items():
        out[name] = (out[name] * factor).astype(out[name].dtype)
    return out
```

```python
from contextlib import ExitStack

import numpy as np
import concourse.bass as bass
from concourse import mybir

F32 = mybir.dt.float32
F32R = mybir.dt.float32r
ALU = mybir.AluOpType
ACT = mybir.ActivationFunctionType
AX = mybir.AxisListType
ds = bass.ds

P = 128
B, SEQ, D = 8, 256, 128
T = B * SEQ
NT = T // P
CH = 512
NCH = T // CH
H, DH, DL = 16, 64, 64
NP = H // 2
E, INTER, K_EXP = 64, 64, 6
G, K_GRP = 8, 4
NPAIR = 1 + E // 2
WCOL = 512
LN_EPS = 1e-5
QK_SCALE = DH ** -0.5
TAKEN = -3e38
FILLER = -2e38
SWAP = [i ^ 1 for i in range(32)]


def bcast(ap, axis, n):
    return ap.unsqueeze(axis).to_broadcast([*ap.shape[:axis], n, *ap.shape[axis:]])


def wait(eng, sem, value):
    if isinstance(value, int) and value <= 0:
        return
    eng.wait_ge(sem, value)


def chunks(eng):
    yield 0
    with eng.Fori(1, NCH) as c:
        yield c


def batches(eng):
    yield 0
    with eng.Fori(1, B - 1) as b:
        yield b
    yield B - 1


def steps(eng):
    for b in batches(eng):
        for j in range(NP):
            yield b * NP + j, b, j


def later(b, j, by):
    if j + by < 0:
        return None if isinstance(b, int) and b == 0 else (b - 1, j + by + NP)
    if j + by >= NP:
        return None if isinstance(b, int) and b == B - 1 else (b + 1, j + by - NP)
    return b, j + by


def pairs(eng):
    yield 0, 0
    yield 1, 1
    yield 2, 0
    with eng.Fori(1, (NPAIR - 1) // 2) as i:
        yield 2 * i + 1, 1
        yield 2 * i + 2, 0


def adaln_kernel(nc, io, out):
    ctx = ExitStack()
    with ctx:
        attn_mem, moe_mem = ExitStack(), ExitStack()

        def sb(name, shape, dt=F32, where=ctx):
            return where.enter_context(nc.sbuf_tensor(name, shape, dt))

        def sem(name):
            return ctx.enter_context(nc.semaphore(name))

        x_sb = sb("x_sb", [P, NT, D])
        mod = sb("mod", [P, B, 6, D])
        ident = sb("ident", [P, P])
        gate_w = sb("gate_w", [P, E])
        gate_b = sb("gate_b", [P, E])
        w_raw = [sb(f"w_raw{i}", [P, WCOL]) for i in range(2)]
        w_hi = [sb(f"w_hi{i}", [P, WCOL], F32R) for i in range(2)]
        w_lo = [sb(f"w_lo{i}", [P, WCOL], F32R) for i in range(2)]
        stats = sb("stats", [P, 4, 6])
        mv = sb("mv", [P, 4, 2])
        var_eps = sb("var_eps", [P, 4])
        rstd = sb("rstd", [P, 4])
        unused = sb("unused", [P, 1])
        one = sb("one", [P, 1])
        minus_half = sb("minus_half", [P, 4])

        with attn_mem:
            def asb(name, shape, dt=F32):
                return sb(name, shape, dt, attn_mem)
            h0 = asb("h0", [P, NT, D])
            cq = asb("cq", [P, T], F32R)
            ckv = asb("ckv", [P, T], F32R)
            ckv_tok = asb("ckv_tok", [P, NT, DL])
            hT = asb("hT", [P, CH])
            hn = asb("hn", [P, 4, D])
            w_down = asb("w_down", [P, 2, 2 * DL])
            w_up = asb("w_up", [P, 2, H * DH])
            w_up_hi = asb("w_up_hi", [P, 2, H * DH], F32R)
            w_up_lo = asb("w_up_lo", [P, 2, H * DH], F32R)
            wv_diag = asb("wv_diag", [P, NP, P])
            wo_t = asb("wo_t", [P, NP, D])
            w_vo = asb("w_vo", [P, NP, D])
            ln_col = asb("ln_col", [P, 2])
            c_t = asb("c_t", [P, B])
            c_rep = asb("c_rep", [P, B, P])
            w_mod = asb("w_mod", [P, 6 * D])
            rope = asb("rope", [P, 2, SEQ])
            swapped = [asb(f"swapped{i}", [P, CH]) for i in range(2)]
            scaled = [asb(f"scaled{i}", [P, CH]) for i in range(2)]
            qk = [asb(f"qk{i}", [P, CH]) for i in range(4)]
            row_max = [asb(f"row_max{i}", [P, 4]) for i in range(2)]
            neg_max = [asb(f"neg_max{i}", [P, 4]) for i in range(2)]
            row_sum = [asb(f"row_sum{i}", [P, 4]) for i in range(2)]
            inv_sum = [asb(f"inv_sum{i}", [P, 4]) for i in range(2)]
            probs = [asb(f"probs{i}", [P, 4, SEQ]) for i in range(2)]
            probs_t = [asb(f"probs_t{i}", [P, 2, CH]) for i in range(2)]
            gate_sign = asb("gate_sign", [P, B, D])
            gate_size = asb("gate_size", [P, B, D])
            kv_now = asb("kv_now", [P, 2, DL])
            mix_t = [asb(f"mix_t{i}", [P, SEQ]) for i in range(2)]
            att_y = asb("att_y", [P, 2, D])
        with moe_mem:
            def msb(name, shape, dt=F32):
                return sb(name, shape, dt, moe_mem)
            h2 = msb("h2", [P, NT, D])
            h2_t = msb("h2_t", [P, T])
            h2_hi = msb("h2_hi", [P, T], F32R)
            h2_lo = msb("h2_lo", [P, T], F32R)
            comb_s = msb("comb_s", [P, T], F32R)
            ones = msb("ones", [P, CH], F32R)
            scores = msb("scores", [P, NT, E + 8])
            chosen = msb("chosen", [P, NT, E + 8])
            grp = msb("grp", [P, NT, 2 * G])
            grp_chosen = msb("grp_chosen", [P, NT, 2 * G])
            grp_top = msb("grp_top", [P, NT, 8])
            grp_mask = msb("grp_mask", [P, NT, G])
            exp_top = msb("exp_top", [P, NT, 8])
            comb = msb("comb", [P, NT, E])
            comb_sum = msb("comb_sum", [P, NT])
            comb_inv = msb("comb_inv", [P, NT])
            comb_2 = msb("comb_2", [P, NT, 2 * E])
            silu_g = [msb(f"silu_g{i}", [P, CH]) for i in range(4)]
            h_u = [msb(f"h_u{i}", [P, CH]) for i in range(4)]
            h_e = [msb(f"h_e{i}", [P, CH]) for i in range(4)]
            h_hi = [msb(f"h_hi{i}", [P, CH], F32R) for i in range(4)]
            h_lo = [msb(f"h_lo{i}", [P, CH], F32R) for i in range(4)]
            y_t = [msb(f"y_t{i}", [P, CH]) for i in range(2)]
            y = [msb(f"y{i}", [P, 4, D]) for i in range(2)]

        ps = ctx.enter_context(nc.psum_tensor("ps", [P, 8, CH], F32))
        up_ps = [ps[:, i, :] for i in range(2)]
        s_ps = ps[:, 2:4, :].rearrange("p h (c k) -> p (h c) k", c=2)
        t_ps = [ps[:, 4 + i, :] for i in range(2)]
        o_ps = ps[:, 6, :]
        f_ps = ps[:, 7, 0:2 * D]
        acc = [ps[:, 4 + i, :] for i in range(4)]

        def ring(u, c, r):
            return ps[:, (3 * c + r) % 4, :]

        in_names = ("x", "c_t", "w_mod", "w_down", "w_up", "wv_diag", "wo_t", "ln_col", "rope",
                    "ident", "gate_w", "gate_b")
        in_x = [sem(f"in_x{c}") for c in range(NCH)]
        in_s = {n: sem("in_" + n) for n in in_names[1:]}
        in_w = [sem("in_w_even"), sem("in_w_odd")]
        (c_silu, c_spread, mod_mm, mod_copied, mod_one, w_up_split_hi, w_up_split,
         wvo_mm, wvo_ready) = map(sem, (
            "c_silu", "c_spread", "mod_mm", "mod_copied", "mod_one", "w_up_split_hi", "w_up_split",
            "wvo_mm", "wvo_ready"))
        st_a, ag_a, nm_a, ml_a, h0_ready, st_b, ag_b, hn_ready, hT_mm, hT_ready, \
            lat_mm, cq_hi, ckv_hi, ckvt_ready, cq_ready, ckv_ready = map(sem, (
                "st_a", "ag_a", "nm_a", "ml_a", "h0_ready", "st_b", "ag_b", "hn_ready",
                "hT_mm", "hT_ready", "lat_mm", "cq_hi", "ckv_hi", "ckvt_ready", "cq_ready", "ckv_ready"))
        up_mm, scaled_ready, swap_ready, sin_done, qk_ready, s_mm, max_ready, neg_ready, exp_done, \
            inv_ready, probs_ready, t_mm, t0_copied, t1_copied, kv_ready, pv_mm, mix_ready, fin_mm, \
            fin_copied, gated, x2_ready = map(sem, (
                "up_mm", "scaled_ready", "swap_ready", "sin_done", "qk_ready", "s_mm", "max_ready",
                "neg_ready", "exp_done", "inv_ready", "probs_ready", "t_mm", "t0_copied", "t1_copied",
                "kv_ready", "pv_mm", "mix_ready", "fin_mm", "fin_copied", "gated", "x2_ready"))
        rs_a, rs_b, rs_c = ([sem(f"var_{k}"), sem(f"rstd_{k}")] for k in "abc")
        half_ready, gate_step = sem("half_ready"), sem("gate_step")
        st_c, ag_c, nm_c, ml_c, h2_ready, h2t_mm, h2t_ready, h2hi_ready, h2lo_ready = map(sem, (
            "st_c", "ag_c", "nm_c", "ml_c", "h2_ready", "h2t_mm", "h2t_ready", "h2hi_ready",
            "h2lo_ready"))
        filler_ready, logit_mm, sig_ready, sc_ready, gm_ready, gtop, gtop_set, gpick, gmask_ready, \
            masked_ready, etop, etop_set, epick, comb_ready, csum_ready, ceps, cinv, comb2_ready, \
            combt_mm, comb_hi, combs_ready, ones_ready = map(sem, (
                "filler_ready", "logit_mm", "sig_ready", "sc_ready", "gm_ready", "gtop", "gtop_set",
                "gpick", "gmask_ready", "masked_ready", "etop", "etop_set", "epick", "comb_ready",
                "csum_ready", "ceps", "cinv", "comb2_ready", "combt_mm", "comb_hi", "combs_ready",
                "ones_ready"))
        whi_gu, wsplit_gu, whi_d, wsplit_d, gate_mm, upx_mm, sel_mm, silu_ready, hu_ready, he_ready, \
            hhi_ready, hlo_ready, down_mm = map(sem, (
                "whi_gu", "wsplit_gu", "whi_d", "wsplit_d", "gate_mm", "upx_mm", "sel_mm",
                "silu_ready", "hu_ready", "he_ready", "hhi_ready", "hlo_ready", "down_mm"))
        yt_ready, y_mm, y_gated, y_ready, stored = map(sem, (
            "yt_ready", "y_mm", "y_gated", "y_ready", "stored"))

        block = ctx.enter_context(nc.Block())

        @block.sync
        def _(sp):
            sp.dma_start(c_t[:, :], io["c_t"]).then_inc(in_s["c_t"], 16)
            sp.dma_start(w_mod[:, :], io["w_mod"]).then_inc(in_s["w_mod"], 16)
            xv = io["x"].rearrange("(c t p) d -> c p t d", c=NCH, p=P)
            for c in range(NCH):
                sp.dma_start(x_sb[:, 4 * c:4 * c + 4, :], xv[c]).then_inc(in_x[c], 16)
            for name, tile in (("ident", ident), ("ln_col", ln_col), ("w_down", w_down), ("w_up", w_up),
                               ("rope", rope), ("wv_diag", wv_diag), ("wo_t", wo_t),
                               ("gate_w", gate_w)):
                t = tile[(slice(None),) * len(tile.shape)]
                sp.dma_start(t, io[name]).then_inc(in_s[name], 16)
            sp.dma_start(gate_b[:, :], io["gate_b"].to_broadcast([P, E])).then_inc(in_s["gate_b"], 16)
            for p, par in pairs(sp):
                wait(sp, wsplit_d, p - 1)
                sp.dma_start(w_raw[par][:, :], io["w_pairs"][ds(p, 1)].rearrange("o p n -> (o p) n")
                             ).then_inc(in_w[par], 16)
            ov = out.rearrange("(c t p) d -> c p t d", c=NCH, p=P)
            for c in range(NCH):
                sp.wait_ge(y_ready, c + 1)
                sp.dma_start(ov[c], y[c % 2][:, :, :]).then_inc(stored, 16)
                sp.wait_ge(stored, 16 * (c + 1))

        @block.tensor
        def _(pe):
            pe.wait_ge(c_spread, 1)
            pe.wait_ge(in_s["w_mod"], 16)
            for b in range(B):
                wait(pe, mod_copied, b - 1)
                k = 2 * (b % 2)
                pe.matmul(ps[:, k, :], c_rep[:, b, :], w_mod[:, 0:CH], start=True, stop=True)
                pe.matmul(ps[:, k + 1, 0:2 * D], c_rep[:, b, :], w_mod[:, CH:6 * D],
                          start=True, stop=True).then_inc(mod_mm, 1)
            pe.wait_ge(in_s["wv_diag"], 16)
            pe.wait_ge(in_s["wo_t"], 16)
            for j in range(NP):
                mm = pe.matmul(ps[:, 4 + j // 4, (j % 4) * D:(j % 4 + 1) * D], wv_diag[:, j, :],
                               wo_t[:, j, :], start=True, stop=True)
            mm.then_inc(wvo_mm, 1)

            pe.wait_ge(in_s["ident"], 16)
            pe.wait_ge(in_s["w_down"], 16)
            pe.wait_ge(mod_copied, B)
            pe.wait_ge(wvo_ready, 1)
            for c in chunks(pe):
                pe.wait_ge(hn_ready, 4 * c + 4)
                for k in range(4):
                    mm = pe.transpose(ps[:, 0, k * P:(k + 1) * P], hn[:, k, :], ident[:, :])
                mm.then_inc(hT_mm, 1)
                pe.wait_ge(hT_ready, c + 1)
                wait(pe, cq_ready, c)
                wait(pe, ckv_ready, c)
                wait(pe, ckvt_ready, c)
                pe.matmul(ps[:, 1, :], w_down[:, 0, :], hT[:, :], start=True, stop=True)
                pe.matmul(ps[:, 2, :], w_down[:, 1, :], hT[:, :], start=True, stop=True)
                for k in range(4):
                    mm = pe.matmul(ps[:, 3, k * DL:(k + 1) * DL], hT[:, k * P:(k + 1) * P],
                                   w_down[:, 1, 0:DL], start=True, stop=True)
                mm.then_inc(lat_mm, 1)

            pe.wait_ge(cq_ready, NCH)
            pe.wait_ge(ckv_ready, NCH)
            pe.wait_ge(ckvt_ready, NCH)
            pe.wait_ge(w_up_split, 1)

            def project(n, b, j):
                wait(pe, swap_ready, n - 1)
                for half, lat in ((0, cq), (1, ckv)):
                    for w in (w_up_hi, w_up_lo):
                        mm = pe.matmul(up_ps[j % 2][:, half * SEQ:(half + 1) * SEQ],
                                       w[:, half, j * P:(j + 1) * P], lat[:, ds(b * SEQ, SEQ)],
                                       start=(w is w_up_hi), stop=(w is w_up_lo))
                mm.then_inc(up_mm, 1)

            def score(n, b, j):
                pe.wait_ge(qk_ready, n + 1)
                wait(pe, exp_done, 4 * n)
                for qh in range(2):
                    for h in range(2):
                        r = slice(DH * h, DH * (h + 1))
                        mm = pe.matmul(s_ps[:, 2 * h + qh, :], qk[j % 4][r, qh * P:(qh + 1) * P],
                                       qk[j % 4][r, SEQ:2 * SEQ], start=True, stop=True)
                mm.then_inc(s_mm, 1)

            def turn(n, b, j):
                pe.wait_ge(probs_ready, n + 1)
                wait(pe, t0_copied, n)
                wait(pe, t1_copied, n)
                for h in range(2):
                    for kh in range(2):
                        for qh in range(2):
                            at = kh * SEQ + qh * P
                            mm = pe.transpose(t_ps[h][:, at:at + P],
                                              probs[j % 2][:, 2 * h + qh, kh * P:(kh + 1) * P], ident[:, :])
                    mm.then_inc(t_mm, 1)

            def mix(n, b, j):
                pe.wait_ge(t0_copied, n + 1)
                pe.wait_ge(t1_copied, n + 1)
                pe.wait_ge(kv_ready, b + 1)
                wait(pe, mix_ready, n)
                for kh in range(2):
                    for h in range(2):
                        mm = pe.matmul(o_ps[DL * h:DL * (h + 1), 0:SEQ], kv_now[:, kh, :],
                                       probs_t[j % 2][:, h, kh * SEQ:(kh + 1) * SEQ],
                                       start=(kh == 0), stop=(kh == 1))
                mm.then_inc(pv_mm, 1)

            def finish(n, b, j):
                pe.wait_ge(mix_ready, n + 1)
                if j == 0:
                    wait(pe, fin_copied, b)
                for qh in range(2):
                    mm = pe.matmul(f_ps[:, qh * D:(qh + 1) * D], mix_t[j % 2][:, qh * P:(qh + 1) * P],
                                   w_vo[:, j, :], start=(j == 0 and qh == 0), stop=(j == NP - 1),
                                   skip_group_check=True)
                mm.then_inc(fin_mm, 1)

            for n in range(3):
                project(n, 0, n)
            score(0, 0, 0)
            for n, b, j in steps(pe):
                for stage, by in ((score, 1), (mix, -1), (finish, -2), (project, 3), (turn, 0)):
                    at = later(b, j, by)
                    if at:
                        stage(n + by, *at)
            mix(B * NP - 1, B - 1, NP - 1)
            finish(B * NP - 2, B - 1, NP - 2)
            finish(B * NP - 1, B - 1, NP - 1)

            pe.wait_ge(fin_copied, B)
            for c in range(NCH):
                pe.wait_ge(h2_ready, c + 1)
                for k in range(4):
                    mm = pe.transpose(ps[:, c, k * P:(k + 1) * P], h2[:, 4 * c + k, :], ident[:, :])
                mm.then_inc(h2t_mm, 1)
            pe.wait_ge(in_s["gate_w"], 16)
            for c in range(NCH):
                pe.wait_ge(h2t_ready, c + 1)
                for k in range(4):
                    t = 4 * c + k
                    mm = pe.matmul(ps[:, 4 + t // 8, (t % 8) * E:(t % 8 + 1) * E],
                                   h2_t[:, t * P:(t + 1) * P], gate_w[:, :], start=True, stop=True)
            mm.then_inc(logit_mm, 1)

            def product(bank, w, par, cols, c, first=True, last=True):
                for a, x, k in ((w_hi, h2_hi, 0), (w_hi, h2_lo, 1), (w_lo, h2_hi, 2)):
                    mm = pe.matmul(bank, a[par][:, cols], x[:, c * CH:(c + 1) * CH],
                                   start=(k == 0), stop=(k == 2))
                return mm

            def down(u, c, par, first, last):
                pe.wait_ge(hlo_ready, u + 1)
                wcols = slice(384, 512)
                for a, x, k in ((w_hi, h_hi, 0), (w_hi, h_lo, 1), (w_lo, h_hi, 2)):
                    mm = pe.matmul(acc[c], a[par][:, wcols], x[c][:, :], start=(first and k == 0),
                                   stop=(last and k == 2), skip_group_check=True)
                mm.then_inc(down_mm, 1)

            pe.wait_ge(h2lo_ready, NCH)
            pe.wait_ge(sig_ready, 1)
            pe.wait_ge(ones_ready, 1)
            for p, par in pairs(pe):
                shared = isinstance(p, int) and p == 0
                pe.wait_ge(wsplit_gu, p + 1)
                for c in range(NCH):
                    u = p * NCH + c
                    wait(pe, he_ready, u - 1)
                    product(ring(u, c, 0), None, par, slice(0, 128), c).then_inc(gate_mm, 1)
                    wait(pe, silu_ready, u)
                    product(ring(u, c, 1), None, par, slice(128, 256), c).then_inc(upx_mm, 1)
                    wait(pe, hu_ready, u)
                    right = ones[:, :] if shared else comb_s[:, c * CH:(c + 1) * CH]
                    pe.matmul(ring(u, c, 2), w_hi[par][:, 256:384], right, start=True,
                              stop=True).then_inc(sel_mm, 1)
                    if shared and c < 2:
                        continue
                    if c == (2 if shared else 0):
                        pe.wait_ge(wsplit_d, p + 1 if shared else p)
                    down(u - 2, (c - 2) % 4, par if c >= 2 else 1 - par,
                         isinstance(p, int) and u - 2 < NCH, False)
                if shared:
                    pe.wait_ge(comb2_ready, 1)
                    pe.wait_ge(he_ready, NCH)
                    for k in range(NCH):
                        for i in range(4):
                            mm = pe.transpose(ps[:, k, i * P:(i + 1) * P], comb_2[:, 4 * k + i, :],
                                              ident[:, :])
                        mm.then_inc(combt_mm, 1)
                    pe.wait_ge(combs_ready, NCH)
            U = NPAIR * NCH
            down(U - 2, 2, 0, False, True)
            down(U - 1, 3, 0, False, True)
            for c in range(NCH):
                pe.wait_ge(yt_ready, c + 1)
                for k in range(4):
                    mm = pe.transpose(ps[:, c, k * P:(k + 1) * P], y_t[c % 2][:, k * P:(k + 1) * P],
                                      ident[:, :])
                mm.then_inc(y_mm, 1)

        @block.vector
        def _(dve):
            def wait_by_memset(sem, value):
                dve.wait_ge(sem, value)
                dve.memset(unused[:, :], 0.0)

            def layernorm_stats(src, t0, st, ag, rs, done):
                for k in range(4):
                    dve.bn_stats(stats[:, k, :], src(k)).then_inc(st, 1)
                wait_by_memset(st, 4 * done + 4)
                for k in range(4):
                    dve.bn_aggr(mv[:, k, :], stats[:, k, :]).then_inc(ag, 1)
                dve.wait_ge(ag, 4 * done + 4)
                dve.tensor_scalar(var_eps[:, :], mv[:, :, 1], LN_EPS, None, ALU.add).then_inc(rs[0], 1)
                dve.wait_ge(rs[1], done + 1)

            dve.wait_ge(c_silu, 1)
            dve.tensor_copy(c_rep[:, :, :], c_t[:, :].unsqueeze(2).to_broadcast([P, B, P])
                            ).then_inc(c_spread, 1)
            dve.wait_ge(w_up_split_hi, 1)
            dve.tensor_tensor(w_up_lo[:, :, :], w_up[:, :, :], w_up_hi[:, :, :], ALU.subtract
                              ).then_inc(w_up_split, 1)
            dve.wait_ge(wvo_mm, 1)
            dve.tensor_copy(w_vo[:, :, :], ps[:, 4:6, :].rearrange("p a (b d) -> p (a b) d", d=D)
                            ).then_inc(wvo_ready, 1)
            for c in range(NCH):
                dve.wait_ge(in_x[c], 16)
            dve.wait_ge(mod_one, 1)
            for c in chunks(dve):
                layernorm_stats(lambda k: x_sb[:, ds(c * 4 + k, 1), :], 0, st_a, ag_a, rs_a, c)
                for k in range(4):
                    dve.tensor_scalar(h0[:, ds(c * 4 + k, 1), :], x_sb[:, ds(c * 4 + k, 1), :],
                                      mv[:, k, 0:1], rstd[:, k:k + 1], ALU.subtract, ALU.mult
                                      ).then_inc(nm_a, 1)
                dve.wait_ge(nm_a, 4 * c + 4)
                h0c = h0[:, ds(c * 4, 4), :].rearrange("p (b t) d -> p b t d", t=2)
                dve.tensor_tensor(h0c, h0c, bcast(mod[:, ds(c * 2, 2), 1, :], 2, 2), ALU.mult
                                  ).then_inc(ml_a, 1)
                dve.wait_ge(ml_a, c + 1)
                dve.tensor_tensor(h0c, h0c, bcast(mod[:, ds(c * 2, 2), 0, :], 2, 2), ALU.add
                                  ).then_inc(h0_ready, 1)
                wait_by_memset(h0_ready, c + 1)
                layernorm_stats(lambda k: h0[:, ds(c * 4 + k, 1), :], 0, st_b, ag_b, rs_b, c)
                wait(dve, hT_mm, c)
                for k in range(4):
                    dve.tensor_scalar(hn[:, k:k + 1, :], h0[:, ds(c * 4 + k, 1), :],
                                      mv[:, k, 0:1], rstd[:, k:k + 1], ALU.subtract, ALU.mult
                                      ).then_inc(hn_ready, 1)
                for bank, lat, hi, ready in ((1, cq, cq_hi, cq_ready), (2, ckv, ckv_hi, ckv_ready)):
                    dve.wait_ge(hi, c + 1)
                    dve.tensor_tensor(lat[DL:P, ds(c * CH, CH)], ps[DL:P, bank, :],
                                      lat[DL:P, ds(c * CH, CH)], ALU.subtract).then_inc(ready, 1)

            dve.wait_ge(in_s["rope"], 16)

            def rotate(n, b, j):
                dve.wait_ge(up_mm, n + 1)
                wait(dve, qk_ready, n - 1)
                dve.tensor_tensor(scaled[j % 2][:, :].rearrange("p (a t) -> p a t", a=2),
                                  up_ps[j % 2].rearrange("p (a t) -> p a t", a=2),
                                  bcast(rope[:, 0, :], 1, 2), ALU.mult).then_inc(scaled_ready, 1)
                dve.stream_shuffle(swapped[j % 2][:, :], up_ps[j % 2], SWAP).then_inc(swap_ready, 1)

            def maximum(n, b, j):
                dve.wait_ge(s_mm, n + 1)
                dve.tensor_reduce(row_max[j % 2][:, :], s_ps, AX.X, ALU.max).then_inc(max_ready, 1)
                dve.wait_ge(max_ready, n + 1)
                dve.tensor_scalar(neg_max[j % 2][:, :], row_max[j % 2][:, :], -QK_SCALE, None, ALU.mult
                                  ).then_inc(neg_ready, 1)

            def invert(n, b, j):
                dve.wait_ge(exp_done, 4 * n + 4)
                dve.reciprocal(inv_sum[j % 2][:, :], row_sum[j % 2][:, :]).then_inc(inv_ready, 1)

            def copy_t0(n, b, j):
                dve.wait_ge(t_mm, 2 * n + 1)
                wait(dve, pv_mm, n - 1)
                dve.tensor_copy(probs_t[j % 2][:, 0, :], t_ps[0]).then_inc(t0_copied, 1)

            def output(b):
                dve.wait_ge(fin_mm, NP * b + NP)
                wait(dve, x2_ready, b)
                dve.tensor_tensor(att_y[:, :, :], f_ps.rearrange("p (t d) -> p t d", t=2),
                                  h0[:, ds(b * 2, 2), :], ALU.add).then_inc(fin_copied, 1)

            for n in range(3):
                rotate(n, 0, n)
            maximum(0, 0, 0)
            invert(0, 0, 0)
            for n, b, j in steps(dve):
                for stage, by in ((copy_t0, -1), (maximum, 1), (rotate, 3), (invert, 1)):
                    at = later(b, j, by)
                    if at:
                        stage(n + by, *at)
                if j == 1 and not (isinstance(b, int) and b == 0):
                    output(b - 1)
            copy_t0(B * NP - 1, B - 1, NP - 1)
            output(B - 1)

            dve.wait_ge(x2_ready, B)
            for c in range(NCH):
                layernorm_stats(lambda k: x_sb[:, 4 * c + k, :], 0, st_c, ag_c, rs_c, c)
                for k in range(4):
                    dve.tensor_scalar(h2[:, 4 * c + k, :], x_sb[:, 4 * c + k, :],
                                      mv[:, k, 0:1], rstd[:, k:k + 1], ALU.subtract, ALU.mult
                                      ).then_inc(nm_c, 1)
                dve.wait_ge(nm_c, 4 * c + 4)
                h2c = h2[:, 4 * c:4 * c + 4, :].rearrange("p (b t) d -> p b t d", t=2)
                dve.tensor_tensor(h2c, h2c, bcast(mod[:, 2 * c:2 * c + 2, 4, :], 2, 2), ALU.mult
                                  ).then_inc(ml_c, 1)
                dve.wait_ge(ml_c, c + 1)
                dve.tensor_tensor(h2c, h2c, bcast(mod[:, 2 * c:2 * c + 2, 3, :], 2, 2), ALU.add
                                  ).then_inc(h2_ready, 1)
            for c in range(NCH):
                dve.wait_ge(h2t_ready, c + 1)
                dve.tensor_copy(h2_hi[:, c * CH:(c + 1) * CH], h2_t[:, c * CH:(c + 1) * CH]
                                ).then_inc(h2hi_ready, 1)

            dve.wait_ge(filler_ready, 3)
            dve.wait_ge(sig_ready, 1)
            dve.wait_ge(in_s["gate_b"], 16)
            sc = scores[:, :, 0:E]
            dve.tensor_tensor(sc, sc, bcast(gate_b[:, :], 1, NT), ALU.add).then_inc(sc_ready, 1)
            dve.wait_ge(sc_ready, 1)
            dve.tensor_reduce(grp[:, :, 0:G], sc.rearrange("p t (g e) -> p t g e", g=G), AX.X, ALU.max
                              ).then_inc(gm_ready, 1)
            dve.wait_ge(gm_ready, 1)
            for t in range(NT):
                dve.max(grp_top[:, t, :], grp[:, t, 0:G]).then_inc(gtop, 1)
            dve.wait_ge(gtop, NT)
            dve.memset(grp_top[:, :, K_GRP:8], FILLER).then_inc(gtop_set, 1)
            dve.wait_ge(gtop_set, 1)
            for t in range(NT):
                dve.match_replace(grp_chosen[:, t, :], grp_top[:, t, :], grp[:, t, :], TAKEN
                                  ).then_inc(gpick, 1)
            dve.wait_ge(gpick, NT)
            dve.tensor_scalar(grp_mask[:, :, :], grp_chosen[:, :, 0:G], TAKEN, None, ALU.is_equal
                              ).then_inc(gmask_ready, 1)
            dve.wait_ge(gmask_ready, 1)
            dve.tensor_tensor(sc.rearrange("p t (g e) -> p t g e", g=G),
                              sc.rearrange("p t (g e) -> p t g e", g=G),
                              grp_mask[:, :, :].unsqueeze(3).to_broadcast([P, NT, G, E // G]), ALU.mult
                              ).then_inc(masked_ready, 1)
            dve.wait_ge(masked_ready, 1)
            for t in range(NT):
                dve.max(exp_top[:, t, :], scores[:, t, 0:E]).then_inc(etop, 1)
            dve.wait_ge(etop, NT)
            dve.memset(exp_top[:, :, K_EXP:8], FILLER).then_inc(etop_set, 1)
            dve.wait_ge(etop_set, 1)
            for t in range(NT):
                dve.match_replace(chosen[:, t, :], exp_top[:, t, :], scores[:, t, :], TAKEN
                                  ).then_inc(epick, 1)
            dve.wait_ge(epick, NT)
            dve.scalar_tensor_tensor(comb[:, :, :], chosen[:, :, 0:E], TAKEN, sc, ALU.is_equal, ALU.mult
                                     ).then_inc(comb_ready, 1)
            dve.wait_ge(comb_ready, 1)
            dve.tensor_reduce(comb_sum[:, :], comb[:, :, :], AX.X, ALU.add).then_inc(csum_ready, 1)
            dve.wait_ge(csum_ready, 1)
            dve.tensor_scalar(comb_sum[:, :], comb_sum[:, :], 1e-8, None, ALU.add).then_inc(ceps, 1)
            dve.wait_ge(ceps, 1)
            dve.reciprocal(comb_inv[:, :], comb_sum[:, :]).then_inc(cinv, 1)
            dve.wait_ge(cinv, 1)
            for half in range(2):
                ins = dve.tensor_tensor(comb_2[:, :, half * E:(half + 1) * E], comb[:, :, :],
                                        comb_inv[:, :].unsqueeze(2).to_broadcast([P, NT, E]), ALU.mult)
            ins.then_inc(comb2_ready, 1)

            for p, par in pairs(dve):
                for c in range(NCH):
                    u = p * NCH + c
                    dve.wait_ge(upx_mm, u + 1)
                    dve.wait_ge(silu_ready, u + 1)
                    dve.tensor_tensor(h_u[c][:, :], ring(u, c, 1), silu_g[c][:, :], ALU.mult
                                      ).then_inc(hu_ready, 1)
                    dve.wait_ge(sel_mm, u + 1)
                    dve.wait_ge(hu_ready, u + 1)
                    wait(dve, hlo_ready, u - 3)
                    dve.tensor_tensor(h_e[c][:, :], ring(u, c, 2), h_u[c][:, :], ALU.mult
                                      ).then_inc(he_ready, 1)
                if isinstance(p, int) and p == 0:
                    for k in range(NCH):
                        dve.wait_ge(comb_hi, k + 1)
                        cs = comb_s[E:P, k * CH:(k + 1) * CH]
                        dve.tensor_tensor(cs, ps[E:P, k, :], cs, ALU.subtract).then_inc(combs_ready, 1)
            for c in range(NCH):
                dve.wait_ge(y_mm, c + 1)
                wait(dve, stored, 16 * (c - 1))
                dve.tensor_tensor(y[c % 2][:, :, :].rearrange("p (b t) d -> p b t d", t=2),
                                  ps[:, c, :].rearrange("p (b t d) -> p b t d", t=2, d=D),
                                  bcast(mod[:, 2 * c:2 * c + 2, 5, :], 2, 2), ALU.mult
                                  ).then_inc(y_gated, 1)
                dve.wait_ge(y_gated, c + 1)
                dve.tensor_tensor(y[c % 2][:, :, :], y[c % 2][:, :, :], x_sb[:, 4 * c:4 * c + 4, :],
                                  ALU.add).then_inc(y_ready, 1)

        @block.scalar
        def _(act):
            act.wait_ge(in_s["c_t"], 16)
            act.activation(c_t[:, :], c_t[:, :], ACT.Silu).then_inc(c_silu, 1)
            act.wait_ge(in_s["w_up"], 16)
            act.copy(w_up_hi[:, :, :], w_up[:, :, :]).then_inc(w_up_split_hi, 1)
            for b in range(B):
                act.wait_ge(mod_mm, b + 1)
                k = 2 * (b % 2)
                act.copy(mod[:, b, :, :].rearrange("p a d -> p (a d)"),
                         ps[:, k:k + 2, :].rearrange("p a n -> p (a n)")[:, 0:6 * D]
                         ).then_inc(mod_copied, 1)
            act.wait_ge(in_s["ln_col"], 16)
            for c in chunks(act):
                act.wait_ge(hT_mm, c + 1)
                wait(act, lat_mm, c)
                act.activation(hT[:, :], ps[:, 0, :], ACT.Identity, bias=ln_col[:, 1:2],
                               scale=ln_col[:, 0:1]).then_inc(hT_ready, 1)
                act.wait_ge(lat_mm, c + 1)
                act.copy(cq[:, ds(c * CH, CH)], ps[:, 1, :]).then_inc(cq_hi, 1)
                act.copy(ckv[:, ds(c * CH, CH)], ps[:, 2, :]).then_inc(ckv_hi, 1)
                act.copy(ckv_tok[:, ds(c * 4, 4), :], ps[:, 3, 0:4 * DL].rearrange(
                    "p (t d) -> p t d", t=4)).then_inc(ckvt_ready, 1)

            def exponent(n, b, j):
                act.wait_ge(neg_ready, n + 1)
                wait(act, t_mm, 2 * (n - 1))
                wait(act, inv_ready, n - 1)
                for i in range(4):
                    act.activation(probs[j % 2][:, i, :], s_ps[:, i, :], ACT.Exp,
                                   bias=neg_max[j % 2][:, i:i + 1], scale=QK_SCALE,
                                   accum_out=row_sum[j % 2][:, i:i + 1]).then_inc(exp_done, 1)

            def copy_t1(n, b, j):
                act.wait_ge(t_mm, 2 * n + 2)
                wait(act, pv_mm, n - 1)
                act.copy(probs_t[j % 2][:, 1, :], t_ps[1]).then_inc(t1_copied, 1)

            def copy_mix(n, b, j):
                act.wait_ge(pv_mm, n + 1)
                wait(act, fin_mm, n - 1)
                act.copy(mix_t[j % 2][:, :], o_ps[:, 0:SEQ]).then_inc(mix_ready, 1)

            exponent(0, 0, 0)
            for n, b, j in steps(act):
                for stage, by in ((copy_t1, -1), (exponent, 1), (copy_mix, -1)):
                    at = later(b, j, by)
                    if at:
                        stage(n + by, *at)
            copy_t1(B * NP - 1, B - 1, NP - 1)
            copy_mix(B * NP - 1, B - 1, NP - 1)

            for c in range(NCH):
                act.wait_ge(h2t_mm, c + 1)
                act.copy(h2_t[:, c * CH:(c + 1) * CH], ps[:, c, :]).then_inc(h2t_ready, 1)
            act.wait_ge(logit_mm, 1)
            act.activation(scores[:, :, 0:E], ps[:, 4:6, :].rearrange("p a (t e) -> p (a t) e", e=E),
                           ACT.Sigmoid).then_inc(sig_ready, 1)

            def silu(u, c):
                act.wait_ge(gate_mm, u + 1)
                wait(act, hu_ready, u - 3)
                act.activation(silu_g[c][:, :], ring(u, c, 0), ACT.Silu).then_inc(silu_ready, 1)

            def split_high(u, c):
                act.wait_ge(he_ready, u + 1)
                wait(act, down_mm, u - 3)
                act.copy(h_hi[c][:, :], h_e[c][:, :]).then_inc(hhi_ready, 1)

            for p, par in pairs(act):
                first = isinstance(p, int) and p == 0
                for c in range(NCH):
                    silu(p * NCH + c, c)
                    if not (first and c == 0) and not (c == 0 and False):
                        split_high(p * NCH + c - 1, (c - 1) % 4)
                if first:
                    for k in range(NCH):
                        act.wait_ge(combt_mm, k + 1)
                        act.copy(comb_s[:, k * CH:(k + 1) * CH], ps[:, k, :]).then_inc(comb_hi, 1)
            split_high(NPAIR * NCH - 1, 3)
            for c in range(NCH):
                act.wait_ge(down_mm, (NPAIR - 1) * NCH + c + 1)
                wait(act, y_mm, c - 1)
                act.copy(y_t[c % 2][:, :], acc[c]).then_inc(yt_ready, 1)

        @block.gpsimd
        def _(pool):
            pool.memset(minus_half[:, :], -0.5).then_inc(half_ready, 1)
            pool.memset(one[:, :], 1.0).then_inc(half_ready, 1)
            pool.wait_ge(half_ready, 2)

            def copy(to, of):
                return pool.tensor_tensor(to, of, one[:, 0:1].to_broadcast([P, of.shape[1]]), ALU.mult)

            def inverse_root(rs, done):
                pool.wait_ge(rs[0], done + 1)
                pool.tensor_tensor(rstd[:, :], var_eps[:, :], minus_half[:, :], ALU.pow).then_inc(rs[1], 1)

            pool.wait_ge(mod_copied, B)
            for a in (1, 4):
                ins = pool.tensor_scalar(mod[:, :, a, :], mod[:, :, a, :], 1.0, None, ALU.add)
            ins.then_inc(mod_one, 1)
            for c in chunks(pool):
                inverse_root(rs_a, c)
                inverse_root(rs_b, c)
            for i, a in enumerate((2, 5)):
                gate = mod[:, :, a, :]
                sign, size = gate_sign[:, :, :], gate_size[:, :, :]
                for k, step in enumerate((
                        lambda: pool.tensor_scalar(sign, gate, 0.0, 2.0, ALU.is_ge, ALU.mult),
                        lambda: pool.tensor_scalar(sign, sign, 1.0, None, ALU.subtract),
                        lambda: pool.tensor_tensor(size, gate, sign, ALU.mult),
                        lambda: pool.tensor_scalar(size, size, 0.25, None, ALU.max),
                        lambda: pool.tensor_tensor(gate, size, sign, ALU.mult))):
                    step().then_inc(gate_step, 1)
                    pool.wait_ge(gate_step, 5 * i + k + 1)
            pool.wait_ge(in_s["rope"], 16)

            def rotate(n, b, j):
                pool.wait_ge(swap_ready, n + 1)
                sw = swapped[j % 2][:, :].rearrange("p (a t) -> p a t", a=2)
                pool.tensor_tensor(sw, sw, bcast(rope[:, 1, :], 1, 2), ALU.mult).then_inc(sin_done, 1)
                pool.wait_ge(scaled_ready, n + 1)
                pool.wait_ge(sin_done, n + 1)
                wait(pool, s_mm, n - 3)
                pool.tensor_tensor(qk[j % 4][:, :], scaled[j % 2][:, :], swapped[j % 2][:, :], ALU.add
                                   ).then_inc(qk_ready, 1)

            def normalise(n, b, j):
                pool.wait_ge(inv_ready, n + 1)
                pool.tensor_tensor(probs[j % 2][:, :, :], probs[j % 2][:, :, :],
                                   inv_sum[j % 2][:, :].unsqueeze(2).to_broadcast([P, 4, SEQ]), ALU.mult
                                   ).then_inc(probs_ready, 1)

            def residual(b):
                pool.wait_ge(fin_copied, b + 1)
                pool.tensor_tensor(att_y[:, :, :], att_y[:, :, :],
                                   mod[:, ds(b, 1), 2, :].to_broadcast([P, 2, D]), ALU.mult
                                   ).then_inc(gated, 1)
                pool.wait_ge(gated, b + 1)
                pool.tensor_tensor(x_sb[:, ds(b * 2, 2), :], att_y[:, :, :], x_sb[:, ds(b * 2, 2), :],
                                   ALU.add).then_inc(x2_ready, 1)

            for n in range(3):
                rotate(n, 0, n)
            normalise(0, 0, 0)
            for n, b, j in steps(pool):
                for stage, by in ((rotate, 3), (normalise, 1)):
                    at = later(b, j, by)
                    if at:
                        stage(n + by, *at)
                if j == 0:
                    wait(pool, pv_mm, n)
                    copy(kv_now[:, :, :].rearrange("p a d -> p (a d)"),
                         ckv_tok[:, ds(b * 2, 2), :].rearrange("p a d -> p (a d)")).then_inc(kv_ready, 1)
                if j == 2 and not (isinstance(b, int) and b == 0):
                    residual(b - 1)
            residual(B - 1)

            for c in range(NCH):
                inverse_root(rs_c, c)
            pool.wait_ge(fin_mm, B * NP)
            pool.memset(scores[:, :, E:E + 8], FILLER).then_inc(filler_ready, 1)
            pool.memset(grp[:, :, G:2 * G], FILLER).then_inc(filler_ready, 1)
            pool.memset(h_u[0][:, :], 1.0).then_inc(filler_ready, 1)
            pool.wait_ge(filler_ready, 3)
            pool.tensor_copy(ones[:, :], h_u[0][:, :]).then_inc(ones_ready, 1)

            def split_gu(p, par, value):
                pool.wait_ge(in_w[par], value)
                wait(pool, sel_mm, NCH * (p - 1))
                copy(w_hi[par][:, 0:384], w_raw[par][:, 0:384]).then_inc(whi_gu, 1)
                pool.wait_ge(whi_gu, p + 1)
                pool.tensor_tensor(w_lo[par][:, 0:256], w_raw[par][:, 0:256], w_hi[par][:, 0:256],
                                   ALU.subtract).then_inc(wsplit_gu, 1)

            def split_d(p, par):
                wait(pool, down_mm, NCH * (p - 1))
                copy(w_hi[par][:, 384:512], w_raw[par][:, 384:512]).then_inc(whi_d, 1)
                pool.wait_ge(whi_d, p + 1)
                pool.tensor_tensor(w_lo[par][:, 384:512], w_raw[par][:, 384:512], w_hi[par][:, 384:512],
                                   ALU.subtract).then_inc(wsplit_d, 1)

            split_gu(0, 0, 16)
            split_d(0, 0)
            for c in range(NCH):
                pool.wait_ge(h2hi_ready, c + 1)
                cols = slice(c * CH, (c + 1) * CH)
                pool.tensor_tensor(h2_lo[:, cols], h2_t[:, cols], h2_hi[:, cols], ALU.subtract
                                   ).then_inc(h2lo_ready, 1)

            def split_low(u, c):
                pool.wait_ge(hhi_ready, u + 1)
                wait(pool, down_mm, u - 3)
                pool.tensor_tensor(h_lo[c][:, :], h_e[c][:, :], h_hi[c][:, :], ALU.subtract
                                   ).then_inc(hlo_ready, 1)

            split_low(0, 0)
            split_gu(1, 1, 16)
            split_low(1, 1)
            split_low(2, 2)
            split_d(1, 1)
            split_low(3, 3)
            with pool.Fori(0, (NPAIR - 3) // 2) as i:
                for q, par in ((1, 1), (2, 0)):
                    u = (2 * i + q) * NCH
                    split_low(u, 0)
                    split_gu(2 * i + q + 1, 1 - par, 16 * (i + 2))
                    split_low(u + 1, 1)
                    split_low(u + 2, 2)
                    split_d(2 * i + q + 1, 1 - par)
                    split_low(u + 3, 3)
            u = (NPAIR - 2) * NCH
            split_low(u, 0)
            split_gu(NPAIR - 1, 0, 16 * ((NPAIR - 1) // 2 + 1))
            split_low(u + 1, 1)
            split_low(u + 2, 2)
            split_d(NPAIR - 1, 0)
            for k in range(3, 8):
                split_low(u + k, k % 4)


def rope_tables():
    inv = 1.0 / 10000.0 ** (np.arange(0, DH, 2, dtype=np.float32) / DH)
    f = np.outer(np.arange(SEQ, dtype=np.float32), inv)
    cos = np.concatenate([np.cos(f), np.cos(f)], -1)[:, ::2]
    sin = np.concatenate([np.sin(f), np.sin(f)], -1)[:, ::2]
    feat = np.arange(P) % DH
    sign = np.where(feat % 2 == 0, -1.0, 1.0).astype(np.float32)
    return np.stack([cos[:, feat // 2].T, sin[:, feat // 2].T * sign[:, None]], 1).astype(np.float32)


def kernel(**inputs):
    import concourse.bacc as bacc
    from concourse.bass_utils import run_bass_kernel_spmd as run

    a = {k: np.asarray(v) for k, v in inputs.items()}
    f = {}
    f["x"] = a["L0_attn_x"].reshape(T, D)
    f["c_t"] = a["L0_c"].T
    f["w_mod"] = a["L0_wmod"]
    wd = [a["L0_attn_w_down_q"].T, a["L0_attn_w_down_kv"].T]
    f["w_down"] = np.stack([np.concatenate([w, w], 1) for w in wd], 1)
    wu = [a["L0_attn_w_up_q"].T, a["L0_attn_w_up_k"].T]
    f["w_up"] = np.stack([np.concatenate([w, w], 0) for w in wu], 1)
    wv = a["L0_attn_w_up_v"].reshape(NP, 2, DH, DL)
    diag = np.zeros((P, NP, P), np.float32)
    diag[0:DH, :, 0:DL] = wv[:, 0].transpose(1, 0, 2)
    diag[DH:P, :, DL:P] = wv[:, 1].transpose(1, 0, 2)
    f["wv_diag"] = diag
    f["wo_t"] = a["L0_attn_w_out"].T.reshape(NP, P, D).transpose(1, 0, 2)
    f["ln_col"] = np.stack([a["L0_attn_ln_scale"], a["L0_attn_ln_bias"]], 1)
    f["rope"] = rope_tables()
    f["ident"] = np.eye(P, dtype=np.float32)
    f["gate_w"] = a["L0_ffn_gate_w"].T
    f["gate_b"] = a["L0_ffn_gate_bias"].reshape(1, E)
    w = np.zeros((NPAIR, P, WCOL), np.float32)
    w[0, :, 0:128] = a["L0_ffn_sg_w"].T
    w[0, :, 128:256] = a["L0_ffn_su_w"].T
    w[0, :, 256:384] = 1.0 / P
    w[0, :, 384:512] = a["L0_ffn_sd_w"].T
    w[1:, :, 0:128] = a["L0_ffn_eg_w"].reshape(E // 2, P, D).transpose(0, 2, 1)
    w[1:, :, 128:256] = a["L0_ffn_eu_w"].reshape(E // 2, P, D).transpose(0, 2, 1)
    for e in range(E):
        at = slice(256 + INTER * (e % 2), 256 + INTER * (e % 2 + 1))
        w[1 + e // 2, e, at] = 1.0
        w[1 + e // 2, E + e, at] = 1.0
    w[1:, :, 384:512] = a["L0_ffn_ed_w"].transpose(0, 2, 1).reshape(E // 2, P, D)
    f["w_pairs"] = w

    nc = bacc.Bacc("TRN2", target_bir_lowering=False, num_devices=1)
    arrays, io = {}, {}
    for name, v in f.items():
        v = np.ascontiguousarray(v)
        arrays["in_" + name] = v
        io[name] = nc.dram_tensor("in_" + name, v.shape, F32, kind="ExternalInput").ap()
    out = nc.dram_tensor("out_0", (T, D), F32, kind="ExternalOutput").ap()
    adaln_kernel(nc, io, out)
    r = run(nc, [arrays], core_ids=[0])
    return r.results[0]["out_0"].reshape(B, SEQ, D)
```

```python
from contextlib import ExitStack

import numpy as np
import concourse.bass as bass
from concourse import mybir

F32 = mybir.dt.float32
F32R = mybir.dt.float32r
ALU = mybir.AluOpType
ACT = mybir.ActivationFunctionType
AX = mybir.AxisListType
ds = bass.ds

P = 128
B, SEQ, D = 8, 256, 128
T = B * SEQ
NT = T // P
CH = 512
NCH = T // CH
H, DH, DL = 16, 64, 64
NP = H // 2
E, INTER, K_EXP = 64, 64, 6
G, K_GRP = 8, 4
NPAIR = 1 + E // 2
WCOL = 512
LN_EPS = 1e-5
QK_SCALE = DH ** -0.5
TAKEN = -3e38
FILLER = -2e38
SWAP = [i ^ 1 for i in range(32)]


def bcast(ap, axis, n):
    return ap.unsqueeze(axis).to_broadcast([*ap.shape[:axis], n, *ap.shape[axis:]])


def wait(eng, sem, value):
    if isinstance(value, int) and value <= 0:
        return
    eng.wait_ge(sem, value)


def chunks(eng):
    yield 0
    with eng.Fori(1, NCH - 1) as c:
        yield c
    yield NCH - 1


def batches(eng):
    yield 0
    with eng.Fori(1, B - 1) as b:
        yield b
    yield B - 1


def steps(eng):
    for b in batches(eng):
        for j in range(NP):
            yield b * NP + j, b, j


def later(b, j, by):
    if j + by < 0:
        return None if isinstance(b, int) and b == 0 else (b - 1, j + by + NP)
    if j + by >= NP:
        return None if isinstance(b, int) and b == B - 1 else (b + 1, j + by - NP)
    return b, j + by


def pairs(eng):
    yield 0, 0
    yield 1, 1
    yield 2, 0
    with eng.Fori(1, (NPAIR - 1) // 2) as i:
        yield 2 * i + 1, 1
        yield 2 * i + 2, 0


def adaln_kernel(nc, io, out):
    ctx = ExitStack()
    with ctx:
        attn_mem, moe_mem = ExitStack(), ExitStack()

        def sb(name, shape, dt=F32, where=ctx):
            return where.enter_context(nc.sbuf_tensor(name, shape, dt))

        def sem(name):
            return ctx.enter_context(nc.semaphore(name))

        x_sb = sb("x_sb", [P, NT, D])
        mod = sb("mod", [P, B, 6, D])
        ident = sb("ident", [P, P])
        gate_w = sb("gate_w", [P, E])
        gate_b = sb("gate_b", [P, E])
        w_raw = [sb(f"w_raw{i}", [P, WCOL]) for i in range(2)]
        w_hi = [sb(f"w_hi{i}", [P, WCOL], F32R) for i in range(2)]
        w_lo = [sb(f"w_lo{i}", [P, WCOL], F32R) for i in range(2)]
        stats = sb("stats", [P, 8, 6])
        mv = sb("mv", [P, 8, 2])
        var_eps = sb("var_eps", [P, 8])
        rstd = sb("rstd", [P, 8])
        unused = sb("unused", [P, 1])
        one = sb("one", [P, 1])
        minus_half = sb("minus_half", [P, 8])

        with attn_mem:
            def asb(name, shape, dt=F32):
                return sb(name, shape, dt, attn_mem)
            h0 = asb("h0", [P, NT, D])
            cq = asb("cq", [P, T], F32R)
            ckv = asb("ckv", [P, T], F32R)
            ckv_tok = asb("ckv_tok", [P, NT, DL])
            hT = asb("hT", [P, CH])
            hn = asb("hn", [P, 4, D])
            w_down = asb("w_down", [P, 2, 2 * DL])
            w_up = asb("w_up", [P, 2, H * DH])
            w_up_hi = asb("w_up_hi", [P, 2, H * DH], F32R)
            w_up_lo = asb("w_up_lo", [P, 2, H * DH], F32R)
            wv_diag = asb("wv_diag", [P, NP, P])
            wo_t = asb("wo_t", [P, NP, D])
            w_vo = asb("w_vo", [P, NP, D])
            ln_col = asb("ln_col", [P, 2])
            c_t = asb("c_t", [P, B])
            c_rep = asb("c_rep", [P, B, P])
            w_mod = asb("w_mod", [P, 6 * D])
            rope = asb("rope", [P, 2, SEQ])
            swapped = [asb(f"swapped{i}", [P, CH]) for i in range(2)]
            scaled = [asb(f"scaled{i}", [P, CH]) for i in range(2)]
            qk = [asb(f"qk{i}", [P, CH]) for i in range(4)]
            row_max = [asb(f"row_max{i}", [P, 4]) for i in range(2)]
            neg_max = [asb(f"neg_max{i}", [P, 4]) for i in range(2)]
            row_sum = [asb(f"row_sum{i}", [P, 4]) for i in range(2)]
            inv_sum = [asb(f"inv_sum{i}", [P, 4]) for i in range(2)]
            probs = [asb(f"probs{i}", [P, 4, SEQ]) for i in range(2)]
            probs_t = [asb(f"probs_t{i}", [P, 2, CH]) for i in range(2)]
            gate_sign = asb("gate_sign", [P, B, D])
            gate_size = asb("gate_size", [P, B, D])
            kv_now = asb("kv_now", [P, 2, DL])
            mix_t = [asb(f"mix_t{i}", [P, SEQ]) for i in range(2)]
            att_y = asb("att_y", [P, 2, D])
        with moe_mem:
            def msb(name, shape, dt=F32):
                return sb(name, shape, dt, moe_mem)
            h2 = msb("h2", [P, NT, D])
            h2_t = msb("h2_t", [P, T])
            h2_hi = msb("h2_hi", [P, T], F32R)
            h2_lo = msb("h2_lo", [P, T], F32R)
            comb_s = msb("comb_s", [P, T], F32R)
            ones = msb("ones", [P, CH], F32R)
            scores = msb("scores", [P, NT, E + 8])
            chosen = msb("chosen", [P, NT, E + 8])
            grp = msb("grp", [P, NT, 2 * G])
            grp_chosen = msb("grp_chosen", [P, NT, 2 * G])
            grp_top = msb("grp_top", [P, NT, 8])
            grp_mask = msb("grp_mask", [P, NT, G])
            exp_top = msb("exp_top", [P, NT, 8])
            comb = msb("comb", [P, NT, E])
            comb_sum = msb("comb_sum", [P, NT])
            comb_inv = msb("comb_inv", [P, NT])
            comb_2 = msb("comb_2", [P, NT, 2 * E])
            silu_g = [msb(f"silu_g{i}", [P, CH]) for i in range(4)]
            h_u = [msb(f"h_u{i}", [P, CH]) for i in range(4)]
            h_e = [msb(f"h_e{i}", [P, CH]) for i in range(4)]
            h_hi = [msb(f"h_hi{i}", [P, CH], F32R) for i in range(4)]
            h_lo = [msb(f"h_lo{i}", [P, CH], F32R) for i in range(4)]
            y_t = [msb(f"y_t{i}", [P, CH]) for i in range(2)]
            y = [msb(f"y{i}", [P, 4, D]) for i in range(2)]

        ps = ctx.enter_context(nc.psum_tensor("ps", [P, 8, CH], F32))
        up_ps = [ps[:, i, :] for i in range(2)]
        s_ps = ps[:, 2:4, :].rearrange("p h (c k) -> p (h c) k", c=2)
        t_ps = [ps[:, 4 + i, :] for i in range(2)]
        o_ps = ps[:, 6, :]
        f_ps = ps[:, 7, 0:2 * D]
        acc = [ps[:, 4 + i, :] for i in range(4)]

        def ring(u, c, r):
            return ps[:, (3 * c + r) % 4, :]

        in_names = ("x", "c_t", "w_mod", "w_down", "w_up", "wv_diag", "wo_t", "ln_col", "rope",
                    "ident", "gate_w", "gate_b")
        in_x = [sem(f"in_x{c}") for c in range(NCH)]
        in_s = {n: sem("in_" + n) for n in in_names[1:]}
        in_w = [sem("in_w_even"), sem("in_w_odd")]
        (c_silu, c_spread, mod_mm, mod_copied, mod_one, w_up_split_hi, w_up_split,
         wvo_mm, wvo_ready) = map(sem, (
            "c_silu", "c_spread", "mod_mm", "mod_copied", "mod_one", "w_up_split_hi", "w_up_split",
            "wvo_mm", "wvo_ready"))
        st_a, ag_a, nm_a, ml_a, h0_ready, st_b, ag_b, hn_ready, hT_mm, hT_ready, \
            lat_mm, cq_hi, ckv_hi, ckvt_ready, cq_ready, ckv_ready = map(sem, (
                "st_a", "ag_a", "nm_a", "ml_a", "h0_ready", "st_b", "ag_b", "hn_ready",
                "hT_mm", "hT_ready", "lat_mm", "cq_hi", "ckv_hi", "ckvt_ready", "cq_ready", "ckv_ready"))
        up_mm, scaled_ready, swap_ready, sin_done, qk_ready, s_mm, max_ready, neg_ready, exp_done, \
            inv_ready, probs0_ready, probs1_ready, t_mm, t0_copied, t1_copied, kv_ready, pv_mm, mix_ready, fin_mm, \
            fin_copied, gated, x2_ready = map(sem, (
                "up_mm", "scaled_ready", "swap_ready", "sin_done", "qk_ready", "s_mm", "max_ready",
                "neg_ready", "exp_done", "inv_ready", "probs0_ready", "probs1_ready", "t_mm", "t0_copied", "t1_copied",
                "kv_ready", "pv_mm", "mix_ready", "fin_mm", "fin_copied", "gated", "x2_ready"))
        rs_a, rs_b, rs_c = ([sem(f"var_{k}"), sem(f"rstd_{k}")] for k in "abc")
        half_ready, sign_ready, size_ready, gate_ready = map(sem, (
            "half_ready", "sign_ready", "size_ready", "gate_ready"))
        st_c, ag_c, nm_c, ml_c, h2_ready, h2t_mm, h2t_ready, h2hi_ready, h2lo_ready = map(sem, (
            "st_c", "ag_c", "nm_c", "ml_c", "h2_ready", "h2t_mm", "h2t_ready", "h2hi_ready",
            "h2lo_ready"))
        filler_ready, logit_mm, sig_ready, sc_ready, gm_ready, gtop, gtop_set, gpick, gmask_ready, \
            masked_ready, etop, etop_set, epick, comb_ready, csum_ready, ceps, cinv, comb2_ready, \
            combt_mm, comb_hi, combs_ready, ones_ready = map(sem, (
                "filler_ready", "logit_mm", "sig_ready", "sc_ready", "gm_ready", "gtop", "gtop_set",
                "gpick", "gmask_ready", "masked_ready", "etop", "etop_set", "epick", "comb_ready",
                "csum_ready", "ceps", "cinv", "comb2_ready", "combt_mm", "comb_hi", "combs_ready",
                "ones_ready"))
        whi_gu, wsplit_gu, whi_d, wsplit_d, gate_mm, upx_mm, sel_mm, silu_ready, hu_ready, he_ready, \
            hhi_ready, hlo_ready, down_mm = map(sem, (
                "whi_gu", "wsplit_gu", "whi_d", "wsplit_d", "gate_mm", "upx_mm", "sel_mm",
                "silu_ready", "hu_ready", "he_ready", "hhi_ready", "hlo_ready", "down_mm"))
        yt_ready, y_mm, y_gated, y_ready, stored = map(sem, (
            "yt_ready", "y_mm", "y_gated", "y_ready", "stored"))

        block = ctx.enter_context(nc.Block())

        @block.sync
        def _(sp):
            sp.dma_start(c_t[:, :], io["c_t"]).then_inc(in_s["c_t"], 16)
            sp.dma_start(w_mod[:, :], io["w_mod"]).then_inc(in_s["w_mod"], 16)
            xv = io["x"].rearrange("(c t p) d -> c p t d", c=NCH, p=P)
            for c in range(NCH):
                sp.dma_start(x_sb[:, 4 * c:4 * c + 4, :], xv[c]).then_inc(in_x[c], 16)
            for name, tile in (("ident", ident), ("ln_col", ln_col), ("w_down", w_down), ("w_up", w_up),
                               ("rope", rope), ("wv_diag", wv_diag), ("wo_t", wo_t),
                               ("gate_w", gate_w)):
                t = tile[(slice(None),) * len(tile.shape)]
                sp.dma_start(t, io[name]).then_inc(in_s[name], 16)
            sp.dma_start(gate_b[:, :], io["gate_b"].to_broadcast([P, E])).then_inc(in_s["gate_b"], 16)
            for p, par in pairs(sp):
                wait(sp, wsplit_d, p - 1)
                sp.dma_start(w_raw[par][:, :], io["w_pairs"][ds(p, 1)].rearrange("o p n -> (o p) n")
                             ).then_inc(in_w[par], 16)
            ov = out.rearrange("(c t p) d -> c p t d", c=NCH, p=P)
            for c in range(NCH):
                sp.wait_ge(y_ready, c + 1)
                sp.dma_start(ov[c], y[c % 2][:, :, :]).then_inc(stored, 16)
                sp.wait_ge(stored, 16 * (c + 1))

        @block.tensor
        def _(pe):
            pe.wait_ge(c_spread, 1)
            pe.wait_ge(in_s["w_mod"], 16)
            for b in range(B):
                mm = pe.matmul(ps[:, b // 2, (b % 2) * 2 * D:(b % 2 + 1) * 2 * D], c_rep[:, b, :],
                               w_mod[:, 0:2 * D], start=True, stop=True)
                if b % 2:
                    mm.then_inc(mod_mm, 1)
            for b in range(B):
                pe.wait_ge(mod_copied, b + 1)
                pe.matmul(ps[:, b % 4, :], c_rep[:, b, :], w_mod[:, 2 * D:6 * D], start=True,
                          stop=True).then_inc(mod_mm, 1)
            pe.wait_ge(in_s["wv_diag"], 16)
            pe.wait_ge(in_s["wo_t"], 16)
            for j in range(NP):
                mm = pe.matmul(ps[:, 4 + j // 4, (j % 4) * D:(j % 4 + 1) * D], wv_diag[:, j, :],
                               wo_t[:, j, :], start=True, stop=True)
            mm.then_inc(wvo_mm, 1)

            pe.wait_ge(in_s["ident"], 16)
            pe.wait_ge(in_s["w_down"], 16)
            pe.wait_ge(mod_copied, B // 2 + B)
            pe.wait_ge(wvo_ready, 1)
            for c in chunks(pe):
                pe.wait_ge(hn_ready, 4 * c + 4)
                for k in range(4):
                    mm = pe.transpose(ps[:, 0, k * P:(k + 1) * P], hn[:, k, :], ident[:, :])
                mm.then_inc(hT_mm, 1)
                pe.wait_ge(hT_ready, c + 1)
                wait(pe, cq_ready, c)
                wait(pe, ckv_ready, c)
                wait(pe, ckvt_ready, c)
                pe.matmul(ps[:, 1, :], w_down[:, 0, :], hT[:, :], start=True, stop=True)
                pe.matmul(ps[:, 2, :], w_down[:, 1, :], hT[:, :], start=True, stop=True)
                for k in range(4):
                    mm = pe.matmul(ps[:, 3, k * DL:(k + 1) * DL], hT[:, k * P:(k + 1) * P],
                                   w_down[:, 1, 0:DL], start=True, stop=True)
                mm.then_inc(lat_mm, 1)

            pe.wait_ge(cq_ready, NCH)
            pe.wait_ge(ckv_ready, NCH)
            pe.wait_ge(ckvt_ready, NCH)
            pe.wait_ge(w_up_split, 1)

            def project(n, b, j):
                wait(pe, swap_ready, n - 1)
                for half, lat in ((0, cq), (1, ckv)):
                    for w in (w_up_hi, w_up_lo):
                        mm = pe.matmul(up_ps[j % 2][:, half * SEQ:(half + 1) * SEQ],
                                       w[:, half, j * P:(j + 1) * P], lat[:, ds(b * SEQ, SEQ)],
                                       start=(w is w_up_hi), stop=(w is w_up_lo))
                mm.then_inc(up_mm, 1)

            def score(n, b, j):
                pe.wait_ge(qk_ready, n + 1)
                for h in range(2):
                    wait(pe, exp_done, 4 * n - 2 + 2 * h)
                    r = slice(DH * h, DH * (h + 1))
                    for qh in range(2):
                        mm = pe.matmul(s_ps[:, 2 * h + qh, :], qk[j % 4][r, qh * P:(qh + 1) * P],
                                       qk[j % 4][r, SEQ:2 * SEQ], start=True, stop=True)
                    mm.then_inc(s_mm, 1)

            def turn(n, b, j):
                for h in range(2):
                    pe.wait_ge((probs0_ready, probs1_ready)[h], 2 * n + 2 if h == 0 else n + 1)
                    wait(pe, (t0_copied, t1_copied)[h], n)
                    for kh in range(2):
                        for qh in range(2):
                            at = kh * SEQ + qh * P
                            mm = pe.transpose(t_ps[h][:, at:at + P],
                                              probs[j % 2][:, 2 * h + qh, kh * P:(kh + 1) * P], ident[:, :])
                    mm.then_inc(t_mm, 1)

            def mix(n, b, j):
                pe.wait_ge(t0_copied, n + 1)
                pe.wait_ge(t1_copied, n + 1)
                pe.wait_ge(kv_ready, b + 1)
                wait(pe, mix_ready, n)
                for kh in range(2):
                    for h in range(2):
                        mm = pe.matmul(o_ps[DL * h:DL * (h + 1), 0:SEQ], kv_now[:, kh, :],
                                       probs_t[j % 2][:, h, kh * SEQ:(kh + 1) * SEQ],
                                       start=(kh == 0), stop=(kh == 1))
                mm.then_inc(pv_mm, 1)

            def finish(n, b, j):
                pe.wait_ge(mix_ready, n + 1)
                if j == 0:
                    wait(pe, fin_copied, b)
                for qh in range(2):
                    mm = pe.matmul(f_ps[:, qh * D:(qh + 1) * D], mix_t[j % 2][:, qh * P:(qh + 1) * P],
                                   w_vo[:, j, :], start=(j == 0 and qh == 0), stop=(j == NP - 1),
                                   skip_group_check=True)
                mm.then_inc(fin_mm, 1)

            for n in range(3):
                project(n, 0, n)
            score(0, 0, 0)
            for n, b, j in steps(pe):
                for stage, by in ((score, 1), (mix, -1), (finish, -2), (project, 3), (turn, 0)):
                    at = later(b, j, by)
                    if at:
                        stage(n + by, *at)
            mix(B * NP - 1, B - 1, NP - 1)
            finish(B * NP - 2, B - 1, NP - 2)
            finish(B * NP - 1, B - 1, NP - 1)

            pe.wait_ge(fin_copied, B)
            for c in range(NCH):
                pe.wait_ge(h2_ready, c + 1)
                for k in range(4):
                    mm = pe.transpose(ps[:, c, k * P:(k + 1) * P], h2[:, 4 * c + k, :], ident[:, :])
                mm.then_inc(h2t_mm, 1)
            pe.wait_ge(in_s["gate_w"], 16)
            for c in range(NCH):
                pe.wait_ge(h2t_ready, c + 1)
                for k in range(4):
                    t = 4 * c + k
                    mm = pe.matmul(ps[:, 4 + t // 8, (t % 8) * E:(t % 8 + 1) * E],
                                   h2_t[:, t * P:(t + 1) * P], gate_w[:, :], start=True, stop=True)
            mm.then_inc(logit_mm, 1)

            def product(bank, w, par, cols, c, first=True, last=True):
                for a, x, k in ((w_hi, h2_hi, 0), (w_hi, h2_lo, 1), (w_lo, h2_hi, 2)):
                    mm = pe.matmul(bank, a[par][:, cols], x[:, c * CH:(c + 1) * CH],
                                   start=(k == 0), stop=(k == 2))
                return mm

            def down(u, c, par, first, last):
                pe.wait_ge(hlo_ready, u + 1)
                wcols = slice(384, 512)
                for a, x, k in ((w_hi, h_hi, 0), (w_hi, h_lo, 1), (w_lo, h_hi, 2)):
                    mm = pe.matmul(acc[c], a[par][:, wcols], x[c][:, :], start=(first and k == 0),
                                   stop=(last and k == 2), skip_group_check=True)
                mm.then_inc(down_mm, 1)

            pe.wait_ge(h2lo_ready, NCH)
            pe.wait_ge(sig_ready, 1)
            pe.wait_ge(ones_ready, 1)
            for p, par in pairs(pe):
                shared = isinstance(p, int) and p == 0
                pe.wait_ge(wsplit_gu, p + 1)
                for c in range(NCH):
                    u = p * NCH + c
                    wait(pe, he_ready, u - 1)
                    product(ring(u, c, 0), None, par, slice(0, 128), c).then_inc(gate_mm, 1)
                    wait(pe, silu_ready, u)
                    product(ring(u, c, 1), None, par, slice(128, 256), c).then_inc(upx_mm, 1)
                    wait(pe, hu_ready, u)
                    right = ones[:, :] if shared else comb_s[:, c * CH:(c + 1) * CH]
                    pe.matmul(ring(u, c, 2), w_hi[par][:, 256:384], right, start=True,
                              stop=True).then_inc(sel_mm, 1)
                    if shared and c < 2:
                        continue
                    if c == (2 if shared else 0):
                        pe.wait_ge(wsplit_d, p + 1 if shared else p)
                    down(u - 2, (c - 2) % 4, par if c >= 2 else 1 - par,
                         isinstance(p, int) and u - 2 < NCH, False)
                if shared:
                    pe.wait_ge(comb2_ready, 1)
                    pe.wait_ge(he_ready, NCH)
                    for k in range(NCH):
                        for i in range(4):
                            mm = pe.transpose(ps[:, k, i * P:(i + 1) * P], comb_2[:, 4 * k + i, :],
                                              ident[:, :])
                        mm.then_inc(combt_mm, 1)
                    pe.wait_ge(combs_ready, NCH)
            U = NPAIR * NCH
            down(U - 2, 2, 0, False, True)
            down(U - 1, 3, 0, False, True)
            for c in range(NCH):
                pe.wait_ge(yt_ready, c + 1)
                for k in range(4):
                    mm = pe.transpose(ps[:, c, k * P:(k + 1) * P], y_t[c % 2][:, k * P:(k + 1) * P],
                                      ident[:, :])
                mm.then_inc(y_mm, 1)

        @block.vector
        def _(dve):
            def wait_by_memset(sem, value):
                dve.wait_ge(sem, value)
                dve.memset(unused[:, :], 0.0)

            def layernorm_stats(src, k0, st, ag, rs, done):
                for k in range(4):
                    dve.bn_stats(stats[:, k0 + k, :], src(k)).then_inc(st, 1)
                wait_by_memset(st, 4 * done + 4)
                for k in range(4):
                    dve.bn_aggr(mv[:, k0 + k, :], stats[:, k0 + k, :]).then_inc(ag, 1)
                dve.wait_ge(ag, 4 * done + 4)
                dve.tensor_scalar(var_eps[:, k0:k0 + 4], mv[:, k0:k0 + 4, 1], LN_EPS, None, ALU.add
                                  ).then_inc(rs[0], 1)

            def normalise(dst, src, k0, rs, done, ready):
                dve.wait_ge(rs[1], done + 1)
                for k in range(4):
                    dve.tensor_scalar(dst(k), src(k), mv[:, k0 + k, 0:1], rstd[:, k0 + k:k0 + k + 1],
                                      ALU.subtract, ALU.mult).then_inc(ready, 1)

            dve.wait_ge(c_silu, 1)
            dve.tensor_copy(c_rep[:, :, :], c_t[:, :].unsqueeze(2).to_broadcast([P, B, P])
                            ).then_inc(c_spread, 1)
            dve.wait_ge(mod_copied, B // 2)
            dve.tensor_scalar(mod[:, :, 1, :], mod[:, :, 1, :], 1.0, None, ALU.add).then_inc(mod_one, 1)
            for c in range(NCH):
                dve.wait_ge(in_x[c], 16)
            dve.wait_ge(mod_one, 1)

            def latent_low(c):
                for bank, lat, hi, ready in ((1, cq, cq_hi, cq_ready), (2, ckv, ckv_hi, ckv_ready)):
                    dve.wait_ge(hi, c + 1)
                    dve.tensor_tensor(lat[DL:P, ds(c * CH, CH)], ps[DL:P, bank, :],
                                      lat[DL:P, ds(c * CH, CH)], ALU.subtract).then_inc(ready, 1)

            def x_tile(c, k):
                return x_sb[:, ds(c * 4 + k, 1), :]

            def h0_tile(c, k):
                return h0[:, ds(c * 4 + k, 1), :]

            def stats_a(c):
                layernorm_stats(lambda k: x_tile(c, k), 0, st_a, ag_a, rs_a, c)

            stats_a(0)
            for c in chunks(dve):
                normalise(lambda k: h0_tile(c, k), lambda k: x_tile(c, k), 0, rs_a, c, nm_a)
                dve.wait_ge(nm_a, 4 * c + 4)
                h0c = h0[:, ds(c * 4, 4), :].rearrange("p (b t) d -> p b t d", t=2)
                dve.tensor_tensor(h0c, h0c, bcast(mod[:, ds(c * 2, 2), 1, :], 2, 2), ALU.mult
                                  ).then_inc(ml_a, 1)
                dve.wait_ge(ml_a, c + 1)
                dve.tensor_tensor(h0c, h0c, bcast(mod[:, ds(c * 2, 2), 0, :], 2, 2), ALU.add
                                  ).then_inc(h0_ready, 1)
                wait_by_memset(h0_ready, c + 1)
                layernorm_stats(lambda k: h0_tile(c, k), 4, st_b, ag_b, rs_b, c)
                if not (isinstance(c, int) and c > 0):
                    stats_a(c + 1)
                wait(dve, hT_mm, c)
                normalise(lambda k: hn[:, k:k + 1, :], lambda k: h0_tile(c, k), 4, rs_b, c, hn_ready)
                if isinstance(c, int) and c == 0:
                    dve.wait_ge(w_up_split_hi, 1)
                    dve.tensor_tensor(w_up_lo[:, :, :], w_up[:, :, :], w_up_hi[:, :, :], ALU.subtract
                                      ).then_inc(w_up_split, 1)
                    dve.wait_ge(wvo_mm, 1)
                    dve.tensor_copy(w_vo[:, :, :], ps[:, 4:6, :].rearrange("p a (b d) -> p (a b) d", d=D)
                                    ).then_inc(wvo_ready, 1)
                else:
                    latent_low(c - 1)
            latent_low(NCH - 1)
            dve.wait_ge(mod_copied, B // 2 + B)
            dve.tensor_scalar(mod[:, :, 4, :], mod[:, :, 4, :], 1.0, None, ALU.add).then_inc(mod_one, 1)
            for i, a in enumerate((2, 5)):
                gate = mod[:, :, a, :]
                dve.tensor_scalar(gate_sign[:, :, :], gate, 0.0, 0.5, ALU.is_ge, ALU.subtract
                                  ).then_inc(sign_ready, 1)
                dve.wait_ge(sign_ready, i + 1)
                dve.scalar_tensor_tensor(gate_size[:, :, :], gate, 4.0, gate_sign[:, :, :], ALU.mult,
                                         ALU.mult).then_inc(size_ready, 1)
                dve.wait_ge(size_ready, i + 1)
                dve.scalar_tensor_tensor(gate, gate_size[:, :, :], 0.5, gate_sign[:, :, :], ALU.max,
                                         ALU.mult).then_inc(gate_ready, 1)
                dve.wait_ge(gate_ready, i + 1)

            dve.wait_ge(in_s["rope"], 16)

            def rotate(n, b, j):
                dve.wait_ge(up_mm, n + 1)
                wait(dve, qk_ready, n - 1)
                dve.tensor_tensor(scaled[j % 2][:, :].rearrange("p (a t) -> p a t", a=2),
                                  up_ps[j % 2].rearrange("p (a t) -> p a t", a=2),
                                  bcast(rope[:, 0, :], 1, 2), ALU.mult).then_inc(scaled_ready, 1)
                dve.stream_shuffle(swapped[j % 2][:, :], up_ps[j % 2], SWAP).then_inc(swap_ready, 1)

            def maximum(n, b, j):
                for h in range(2):
                    rows = slice(2 * h, 2 * h + 2)
                    dve.wait_ge(s_mm, 2 * n + h + 1)
                    dve.tensor_reduce(row_max[j % 2][:, rows], s_ps[:, rows, :], AX.X, ALU.max
                                      ).then_inc(max_ready, 1)
                    dve.wait_ge(max_ready, 2 * n + h + 1)
                    dve.tensor_scalar(neg_max[j % 2][:, rows], row_max[j % 2][:, rows], -QK_SCALE, None,
                                      ALU.mult).then_inc(neg_ready, 1)

            def invert(n, b, j):
                dve.wait_ge(exp_done, 4 * n + 4)
                dve.reciprocal(inv_sum[j % 2][:, :], row_sum[j % 2][:, :]).then_inc(inv_ready, 1)
                dve.wait_ge(inv_ready, n + 1)
                for i in range(2):
                    dve.tensor_scalar(probs[j % 2][:, i, :], probs[j % 2][:, i, :],
                                      inv_sum[j % 2][:, i:i + 1], None, ALU.mult).then_inc(probs0_ready, 1)

            def copy_t0(n, b, j):
                dve.wait_ge(t_mm, 2 * n + 1)
                wait(dve, pv_mm, n - 1)
                dve.tensor_copy(probs_t[j % 2][:, 0, :], t_ps[0]).then_inc(t0_copied, 1)

            def output(b):
                dve.wait_ge(fin_mm, NP * b + NP)
                dve.wait_ge(x2_ready, b + 1)
                dve.tensor_tensor(att_y[:, :, :], f_ps.rearrange("p (t d) -> p t d", t=2),
                                  h0[:, ds(b * 2, 2), :], ALU.add).then_inc(fin_copied, 1)

            for n in range(3):
                rotate(n, 0, n)
            maximum(0, 0, 0)
            invert(0, 0, 0)
            for n, b, j in steps(dve):
                for stage, by in ((copy_t0, -1), (maximum, 1), (rotate, 3), (invert, 1)):
                    at = later(b, j, by)
                    if at:
                        stage(n + by, *at)
                if j == 1 and not (isinstance(b, int) and b == 0):
                    output(b - 1)
            copy_t0(B * NP - 1, B - 1, NP - 1)
            output(B - 1)

            dve.wait_ge(x2_ready, B + 1)
            dve.wait_ge(mod_one, 2)

            def stats_c(c):
                layernorm_stats(lambda k: x_sb[:, 4 * c + k, :], 4 * (c % 2), st_c, ag_c, rs_c, c)

            for c in range(NCH):
                if c == 0:
                    stats_c(0)
                if c + 1 < NCH:
                    stats_c(c + 1)
                normalise(lambda k: h2[:, 4 * c + k, :], lambda k: x_sb[:, 4 * c + k, :],
                          4 * (c % 2), rs_c, c, nm_c)
                dve.wait_ge(nm_c, 4 * c + 4)
                h2c = h2[:, 4 * c:4 * c + 4, :].rearrange("p (b t) d -> p b t d", t=2)
                dve.tensor_tensor(h2c, h2c, bcast(mod[:, 2 * c:2 * c + 2, 4, :], 2, 2), ALU.mult
                                  ).then_inc(ml_c, 1)
                dve.wait_ge(ml_c, c + 1)
                dve.tensor_tensor(h2c, h2c, bcast(mod[:, 2 * c:2 * c + 2, 3, :], 2, 2), ALU.add
                                  ).then_inc(h2_ready, 1)
            for c in range(NCH):
                dve.wait_ge(h2t_ready, c + 1)
                dve.tensor_copy(h2_hi[:, c * CH:(c + 1) * CH], h2_t[:, c * CH:(c + 1) * CH]
                                ).then_inc(h2hi_ready, 1)

            dve.wait_ge(filler_ready, 3)
            dve.wait_ge(sig_ready, 1)
            dve.wait_ge(in_s["gate_b"], 16)
            sc = scores[:, :, 0:E]
            dve.tensor_tensor(sc, sc, bcast(gate_b[:, :], 1, NT), ALU.add).then_inc(sc_ready, 1)
            dve.wait_ge(sc_ready, 1)
            dve.tensor_reduce(grp[:, :, 0:G], sc.rearrange("p t (g e) -> p t g e", g=G), AX.X, ALU.max
                              ).then_inc(gm_ready, 1)
            dve.wait_ge(gm_ready, 1)
            for t in range(NT):
                dve.max(grp_top[:, t, :], grp[:, t, 0:G]).then_inc(gtop, 1)
            dve.wait_ge(gtop, NT)
            dve.memset(grp_top[:, :, K_GRP:8], FILLER).then_inc(gtop_set, 1)
            dve.wait_ge(gtop_set, 1)
            for t in range(NT):
                dve.match_replace(grp_chosen[:, t, :], grp_top[:, t, :], grp[:, t, :], TAKEN
                                  ).then_inc(gpick, 1)
            dve.wait_ge(gpick, NT)
            dve.tensor_scalar(grp_mask[:, :, :], grp_chosen[:, :, 0:G], TAKEN, None, ALU.is_equal
                              ).then_inc(gmask_ready, 1)
            dve.wait_ge(gmask_ready, 1)
            dve.tensor_tensor(sc.rearrange("p t (g e) -> p t g e", g=G),
                              sc.rearrange("p t (g e) -> p t g e", g=G),
                              grp_mask[:, :, :].unsqueeze(3).to_broadcast([P, NT, G, E // G]), ALU.mult
                              ).then_inc(masked_ready, 1)
            dve.wait_ge(masked_ready, 1)
            for t in range(NT):
                dve.max(exp_top[:, t, :], scores[:, t, 0:E]).then_inc(etop, 1)
            dve.wait_ge(etop, NT)
            dve.memset(exp_top[:, :, K_EXP:8], FILLER).then_inc(etop_set, 1)
            dve.wait_ge(etop_set, 1)
            for t in range(NT):
                dve.match_replace(chosen[:, t, :], exp_top[:, t, :], scores[:, t, :], TAKEN
                                  ).then_inc(epick, 1)
            dve.wait_ge(epick, NT)
            dve.scalar_tensor_tensor(comb[:, :, :], chosen[:, :, 0:E], TAKEN, sc, ALU.is_equal, ALU.mult
                                     ).then_inc(comb_ready, 1)
            dve.wait_ge(comb_ready, 1)
            dve.tensor_reduce(comb_sum[:, :], comb[:, :, :], AX.X, ALU.add).then_inc(csum_ready, 1)
            dve.wait_ge(csum_ready, 1)
            dve.tensor_scalar(comb_sum[:, :], comb_sum[:, :], 1e-8, None, ALU.add).then_inc(ceps, 1)
            dve.wait_ge(ceps, 1)
            dve.reciprocal(comb_inv[:, :], comb_sum[:, :]).then_inc(cinv, 1)
            dve.wait_ge(cinv, 1)
            for half in range(2):
                ins = dve.tensor_tensor(comb_2[:, :, half * E:(half + 1) * E], comb[:, :, :],
                                        comb_inv[:, :].unsqueeze(2).to_broadcast([P, NT, E]), ALU.mult)
            ins.then_inc(comb2_ready, 1)

            for p, par in pairs(dve):
                for c in range(NCH):
                    u = p * NCH + c
                    dve.wait_ge(upx_mm, u + 1)
                    dve.wait_ge(silu_ready, u + 1)
                    dve.tensor_tensor(h_u[c][:, :], ring(u, c, 1), silu_g[c][:, :], ALU.mult
                                      ).then_inc(hu_ready, 1)
                    dve.wait_ge(sel_mm, u + 1)
                    dve.wait_ge(hu_ready, u + 1)
                    wait(dve, hlo_ready, u - 3)
                    dve.tensor_tensor(h_e[c][:, :], ring(u, c, 2), h_u[c][:, :], ALU.mult
                                      ).then_inc(he_ready, 1)
                if isinstance(p, int) and p == 0:
                    for k in range(NCH):
                        dve.wait_ge(comb_hi, k + 1)
                        cs = comb_s[E:P, k * CH:(k + 1) * CH]
                        dve.tensor_tensor(cs, ps[E:P, k, :], cs, ALU.subtract).then_inc(combs_ready, 1)
            for c in range(NCH):
                dve.wait_ge(y_mm, c + 1)
                wait(dve, stored, 16 * (c - 1))
                dve.tensor_tensor(y[c % 2][:, :, :].rearrange("p (b t) d -> p b t d", t=2),
                                  ps[:, c, :].rearrange("p (b t d) -> p b t d", t=2, d=D),
                                  bcast(mod[:, 2 * c:2 * c + 2, 5, :], 2, 2), ALU.mult
                                  ).then_inc(y_gated, 1)
                dve.wait_ge(y_gated, c + 1)
                dve.tensor_tensor(y[c % 2][:, :, :], y[c % 2][:, :, :], x_sb[:, 4 * c:4 * c + 4, :],
                                  ALU.add).then_inc(y_ready, 1)

        @block.scalar
        def _(act):
            act.wait_ge(in_s["c_t"], 16)
            act.activation(c_t[:, :], c_t[:, :], ACT.Silu).then_inc(c_silu, 1)
            for k in range(B // 2):
                act.wait_ge(mod_mm, k + 1)
                act.copy(mod[:, 2 * k:2 * k + 2, 0:2, :].rearrange("p b a d -> p b (a d)"),
                         ps[:, k, :].rearrange("p (b d) -> p b d", b=2)).then_inc(mod_copied, 1)
            for b in range(B):
                act.wait_ge(mod_mm, B // 2 + b + 1)
                act.copy(mod[:, b, 2:6, :].rearrange("p a d -> p (a d)"), ps[:, b % 4, :]
                         ).then_inc(mod_copied, 1)
            act.wait_ge(in_s["w_up"], 16)
            act.copy(w_up_hi[:, :, :], w_up[:, :, :]).then_inc(w_up_split_hi, 1)
            act.wait_ge(in_s["ln_col"], 16)
            for c in chunks(act):
                act.wait_ge(hT_mm, c + 1)
                wait(act, lat_mm, c)
                act.activation(hT[:, :], ps[:, 0, :], ACT.Identity, bias=ln_col[:, 1:2],
                               scale=ln_col[:, 0:1]).then_inc(hT_ready, 1)
                act.wait_ge(lat_mm, c + 1)
                act.copy(cq[:, ds(c * CH, CH)], ps[:, 1, :]).then_inc(cq_hi, 1)
                act.copy(ckv[:, ds(c * CH, CH)], ps[:, 2, :]).then_inc(ckv_hi, 1)
                act.copy(ckv_tok[:, ds(c * 4, 4), :], ps[:, 3, 0:4 * DL].rearrange(
                    "p (t d) -> p t d", t=4)).then_inc(ckvt_ready, 1)

            def exponent(n, b, j):
                wait(act, t_mm, 2 * (n - 1))
                wait(act, inv_ready, n - 1)
                for i in range(4):
                    if i % 2 == 0:
                        act.wait_ge(neg_ready, 2 * n + i // 2 + 1)
                    act.activation(probs[j % 2][:, i, :], s_ps[:, i, :], ACT.Exp,
                                   bias=neg_max[j % 2][:, i:i + 1], scale=QK_SCALE,
                                   accum_out=row_sum[j % 2][:, i:i + 1]).then_inc(exp_done, 1)

            def copy_t1(n, b, j):
                act.wait_ge(t_mm, 2 * n + 2)
                wait(act, pv_mm, n - 1)
                act.copy(probs_t[j % 2][:, 1, :], t_ps[1]).then_inc(t1_copied, 1)

            def copy_mix(n, b, j):
                act.wait_ge(pv_mm, n + 1)
                wait(act, fin_mm, n - 1)
                act.copy(mix_t[j % 2][:, :], o_ps[:, 0:SEQ]).then_inc(mix_ready, 1)

            exponent(0, 0, 0)
            for n, b, j in steps(act):
                for stage, by in ((copy_t1, -1), (exponent, 1), (copy_mix, -1)):
                    at = later(b, j, by)
                    if at:
                        stage(n + by, *at)
            copy_t1(B * NP - 1, B - 1, NP - 1)
            copy_mix(B * NP - 1, B - 1, NP - 1)

            for c in range(NCH):
                act.wait_ge(h2t_mm, c + 1)
                act.copy(h2_t[:, c * CH:(c + 1) * CH], ps[:, c, :]).then_inc(h2t_ready, 1)
            act.wait_ge(logit_mm, 1)
            act.activation(scores[:, :, 0:E], ps[:, 4:6, :].rearrange("p a (t e) -> p (a t) e", e=E),
                           ACT.Sigmoid).then_inc(sig_ready, 1)

            def silu(u, c):
                act.wait_ge(gate_mm, u + 1)
                wait(act, hu_ready, u - 3)
                act.activation(silu_g[c][:, :], ring(u, c, 0), ACT.Silu).then_inc(silu_ready, 1)

            def split_high(u, c):
                act.wait_ge(he_ready, u + 1)
                wait(act, down_mm, u - 3)
                act.copy(h_hi[c][:, :], h_e[c][:, :]).then_inc(hhi_ready, 1)

            for p, par in pairs(act):
                first = isinstance(p, int) and p == 0
                for c in range(NCH):
                    silu(p * NCH + c, c)
                    if not (first and c == 0) and not (c == 0 and False):
                        split_high(p * NCH + c - 1, (c - 1) % 4)
                if first:
                    for k in range(NCH):
                        act.wait_ge(combt_mm, k + 1)
                        act.copy(comb_s[:, k * CH:(k + 1) * CH], ps[:, k, :]).then_inc(comb_hi, 1)
            split_high(NPAIR * NCH - 1, 3)
            for c in range(NCH):
                act.wait_ge(down_mm, (NPAIR - 1) * NCH + c + 1)
                wait(act, y_mm, c - 1)
                act.copy(y_t[c % 2][:, :], acc[c]).then_inc(yt_ready, 1)

        @block.gpsimd
        def _(pool):
            pool.memset(minus_half[:, :], -0.5).then_inc(half_ready, 1)
            pool.memset(att_y[:, :, :], 0.0).then_inc(x2_ready, 1)
            pool.memset(one[:, :], 1.0).then_inc(half_ready, 1)
            pool.wait_ge(half_ready, 2)

            def copy(to, of):
                return pool.tensor_tensor(to, of, one[:, 0:1].to_broadcast([P, of.shape[1]]), ALU.mult)

            def inverse_root(rs, k0, done):
                pool.wait_ge(rs[0], done + 1)
                at = slice(k0, k0 + 4)
                pool.tensor_tensor(rstd[:, at], var_eps[:, at], minus_half[:, at], ALU.pow
                                   ).then_inc(rs[1], 1)

            for c in chunks(pool):
                inverse_root(rs_a, 0, c)
                inverse_root(rs_b, 4, c)
            pool.wait_ge(in_s["rope"], 16)

            def rotate(n, b, j):
                pool.wait_ge(swap_ready, n + 1)
                sw = swapped[j % 2][:, :].rearrange("p (a t) -> p a t", a=2)
                pool.tensor_tensor(sw, sw, bcast(rope[:, 1, :], 1, 2), ALU.mult).then_inc(sin_done, 1)
                pool.wait_ge(scaled_ready, n + 1)
                pool.wait_ge(sin_done, n + 1)
                wait(pool, s_mm, 2 * (n - 3))
                pool.tensor_tensor(qk[j % 4][:, :], scaled[j % 2][:, :], swapped[j % 2][:, :], ALU.add
                                   ).then_inc(qk_ready, 1)

            def normalise(n, b, j):
                pool.wait_ge(inv_ready, n + 1)
                pool.tensor_tensor(probs[j % 2][:, 2:4, :], probs[j % 2][:, 2:4, :],
                                   inv_sum[j % 2][:, 2:4].unsqueeze(2).to_broadcast([P, 2, SEQ]), ALU.mult
                                   ).then_inc(probs1_ready, 1)

            def latents_now(n, b, j):
                if j == 0:
                    wait(pool, pv_mm, n)
                    copy(kv_now[:, :, :].rearrange("p a d -> p (a d)"),
                         ckv_tok[:, ds(b * 2, 2), :].rearrange("p a d -> p (a d)")).then_inc(kv_ready, 1)

            def residual(b):
                pool.wait_ge(gate_ready, 1)
                pool.wait_ge(fin_copied, b + 1)
                pool.tensor_tensor(att_y[:, :, :], att_y[:, :, :],
                                   mod[:, ds(b, 1), 2, :].to_broadcast([P, 2, D]), ALU.mult
                                   ).then_inc(gated, 1)
                pool.wait_ge(gated, b + 1)
                pool.tensor_tensor(x_sb[:, ds(b * 2, 2), :], att_y[:, :, :], x_sb[:, ds(b * 2, 2), :],
                                   ALU.add).then_inc(x2_ready, 1)

            for n in range(3):
                rotate(n, 0, n)
            normalise(0, 0, 0)
            for n, b, j in steps(pool):
                for stage, by in ((rotate, 3), (latents_now, 0), (normalise, 1)):
                    at = later(b, j, by)
                    if at:
                        stage(n + by, *at)
                if j == 2 and not (isinstance(b, int) and b == 0):
                    residual(b - 1)
            residual(B - 1)

            for c in range(NCH):
                inverse_root(rs_c, 4 * (c % 2), c)
            pool.wait_ge(fin_mm, B * NP)
            pool.memset(scores[:, :, E:E + 8], FILLER).then_inc(filler_ready, 1)
            pool.memset(grp[:, :, G:2 * G], FILLER).then_inc(filler_ready, 1)
            pool.memset(h_u[0][:, :], 1.0).then_inc(filler_ready, 1)
            pool.wait_ge(filler_ready, 3)
            pool.tensor_copy(ones[:, :], h_u[0][:, :]).then_inc(ones_ready, 1)

            def split_gu(p, par, value):
                pool.wait_ge(in_w[par], value)
                wait(pool, sel_mm, NCH * (p - 1))
                copy(w_hi[par][:, 0:384], w_raw[par][:, 0:384]).then_inc(whi_gu, 1)
                pool.wait_ge(whi_gu, p + 1)
                pool.tensor_tensor(w_lo[par][:, 0:256], w_raw[par][:, 0:256], w_hi[par][:, 0:256],
                                   ALU.subtract).then_inc(wsplit_gu, 1)

            def split_d(p, par):
                wait(pool, down_mm, NCH * (p - 1))
                copy(w_hi[par][:, 384:512], w_raw[par][:, 384:512]).then_inc(whi_d, 1)
                pool.wait_ge(whi_d, p + 1)
                pool.tensor_tensor(w_lo[par][:, 384:512], w_raw[par][:, 384:512], w_hi[par][:, 384:512],
                                   ALU.subtract).then_inc(wsplit_d, 1)

            split_gu(0, 0, 16)
            split_d(0, 0)
            for c in range(NCH):
                pool.wait_ge(h2hi_ready, c + 1)
                cols = slice(c * CH, (c + 1) * CH)
                pool.tensor_tensor(h2_lo[:, cols], h2_t[:, cols], h2_hi[:, cols], ALU.subtract
                                   ).then_inc(h2lo_ready, 1)

            def split_low(u, c):
                pool.wait_ge(hhi_ready, u + 1)
                wait(pool, down_mm, u - 3)
                pool.tensor_tensor(h_lo[c][:, :], h_e[c][:, :], h_hi[c][:, :], ALU.subtract
                                   ).then_inc(hlo_ready, 1)

            split_low(0, 0)
            split_gu(1, 1, 16)
            split_low(1, 1)
            split_low(2, 2)
            split_d(1, 1)
            split_low(3, 3)
            with pool.Fori(0, (NPAIR - 3) // 2) as i:
                for q, par in ((1, 1), (2, 0)):
                    u = (2 * i + q) * NCH
                    split_low(u, 0)
                    split_gu(2 * i + q + 1, 1 - par, 16 * (i + 2))
                    split_low(u + 1, 1)
                    split_low(u + 2, 2)
                    split_d(2 * i + q + 1, 1 - par)
                    split_low(u + 3, 3)
            u = (NPAIR - 2) * NCH
            split_low(u, 0)
            split_gu(NPAIR - 1, 0, 16 * ((NPAIR - 1) // 2 + 1))
            split_low(u + 1, 1)
            split_low(u + 2, 2)
            split_d(NPAIR - 1, 0)
            for k in range(3, 8):
                split_low(u + k, k % 4)


def rope_tables():
    inv = 1.0 / 10000.0 ** (np.arange(0, DH, 2, dtype=np.float32) / DH)
    f = np.outer(np.arange(SEQ, dtype=np.float32), inv)
    cos = np.concatenate([np.cos(f), np.cos(f)], -1)[:, ::2]
    sin = np.concatenate([np.sin(f), np.sin(f)], -1)[:, ::2]
    feat = np.arange(P) % DH
    sign = np.where(feat % 2 == 0, -1.0, 1.0).astype(np.float32)
    return np.stack([cos[:, feat // 2].T, sin[:, feat // 2].T * sign[:, None]], 1).astype(np.float32)


def kernel(**inputs):
    import concourse.bacc as bacc
    from concourse.bass_utils import run_bass_kernel_spmd as run

    a = {k: np.asarray(v) for k, v in inputs.items()}
    f = {}
    f["x"] = a["L0_attn_x"].reshape(T, D)
    f["c_t"] = a["L0_c"].T
    f["w_mod"] = a["L0_wmod"]
    wd = [a["L0_attn_w_down_q"].T, a["L0_attn_w_down_kv"].T]
    f["w_down"] = np.stack([np.concatenate([w, w], 1) for w in wd], 1)
    wu = [a["L0_attn_w_up_q"].T, a["L0_attn_w_up_k"].T]
    f["w_up"] = np.stack([np.concatenate([w, w], 0) for w in wu], 1)
    wv = a["L0_attn_w_up_v"].reshape(NP, 2, DH, DL)
    diag = np.zeros((P, NP, P), np.float32)
    diag[0:DH, :, 0:DL] = wv[:, 0].transpose(1, 0, 2)
    diag[DH:P, :, DL:P] = wv[:, 1].transpose(1, 0, 2)
    f["wv_diag"] = diag
    f["wo_t"] = a["L0_attn_w_out"].T.reshape(NP, P, D).transpose(1, 0, 2)
    f["ln_col"] = np.stack([a["L0_attn_ln_scale"], a["L0_attn_ln_bias"]], 1)
    f["rope"] = rope_tables()
    f["ident"] = np.eye(P, dtype=np.float32)
    f["gate_w"] = a["L0_ffn_gate_w"].T
    f["gate_b"] = a["L0_ffn_gate_bias"].reshape(1, E)
    w = np.zeros((NPAIR, P, WCOL), np.float32)
    w[0, :, 0:128] = a["L0_ffn_sg_w"].T
    w[0, :, 128:256] = a["L0_ffn_su_w"].T
    w[0, :, 256:384] = 1.0 / P
    w[0, :, 384:512] = a["L0_ffn_sd_w"].T
    w[1:, :, 0:128] = a["L0_ffn_eg_w"].reshape(E // 2, P, D).transpose(0, 2, 1)
    w[1:, :, 128:256] = a["L0_ffn_eu_w"].reshape(E // 2, P, D).transpose(0, 2, 1)
    for e in range(E):
        at = slice(256 + INTER * (e % 2), 256 + INTER * (e % 2 + 1))
        w[1 + e // 2, e, at] = 1.0
        w[1 + e // 2, E + e, at] = 1.0
    w[1:, :, 384:512] = a["L0_ffn_ed_w"].transpose(0, 2, 1).reshape(E // 2, P, D)
    f["w_pairs"] = w

    nc = bacc.Bacc("TRN2", target_bir_lowering=False, num_devices=1)
    arrays, io = {}, {}
    for name, v in f.items():
        v = np.ascontiguousarray(v)
        arrays["in_" + name] = v
        io[name] = nc.dram_tensor("in_" + name, v.shape, F32, kind="ExternalInput").ap()
    out = nc.dram_tensor("out_0", (T, D), F32, kind="ExternalOutput").ap()
    adaln_kernel(nc, io, out)
    r = run(nc, [arrays], core_ids=[0])
    return r.results[0]["out_0"].reshape(B, SEQ, D)
```

```python
from contextlib import ExitStack
from itertools import count

import numpy as np
import concourse.bass as bass
from concourse import mybir

F32 = mybir.dt.float32
F32R = mybir.dt.float32r
ALU = mybir.AluOpType
ACT = mybir.ActivationFunctionType
AX = mybir.AxisListType
ds = bass.ds

P = 128
B, SEQ, D = 8, 256, 128
T = B * SEQ
NT = T // P
CH = 512
NCH = T // CH
H, DH, DL = 16, 64, 64
NP = H // 2
E, INTER, K_EXP = 64, 64, 6
G, K_GRP = 8, 4
NPAIR = 1 + E // 2
WCOL = 512
WVAL = 384
LN_EPS = 1e-5
QK_SCALE = DH ** -0.5
TAKEN = -3e38
FILLER = -2e38
SWAP = [i ^ 1 for i in range(32)]


def bcast(ap, axis, n):
    return ap.unsqueeze(axis).to_broadcast([*ap.shape[:axis], n, *ap.shape[axis:]])


def wait(eng, sem, value):
    if isinstance(value, int) and value <= 0:
        return
    eng.wait_ge(sem, value)


def chunks(eng):
    yield 0
    with eng.Fori(1, NCH - 1) as c:
        yield c
    yield NCH - 1


def batches(eng):
    yield 0
    yield 1
    yield 2
    with eng.Fori(3, B - 1) as b:
        yield b
    yield B - 1


def steps(eng):
    for b in batches(eng):
        for j in range(NP):
            yield b * NP + j, b, j


def later(b, j, by):
    if j + by < 0:
        return None if isinstance(b, int) and b == 0 else (b - 1, j + by + NP)
    if j + by >= NP:
        return None if isinstance(b, int) and b == B - 1 else (b + 1, j + by - NP)
    return b, j + by


def behind(b, by):
    return not isinstance(b, int) or b >= by


def last(b):
    return 1 if isinstance(b, int) and b == B - 1 else 0


def pairs(eng):
    yield 0, 0, 1
    yield 1, 1, 2
    with eng.Fori(1, (NPAIR - 1) // 2) as i:
        yield 2 * i, 0, i + 1
        yield 2 * i + 1, 1, i + 2
    yield NPAIR - 1, 0, None


def adaln_kernel(nc, io, out):
    ctx = ExitStack()
    with ctx:
        attn_mem, ahead_mem, moe_mem = ExitStack(), ExitStack(), ExitStack()

        def sb(name, shape, dt=F32, where=ctx):
            return where.enter_context(nc.sbuf_tensor(name, shape, dt))

        def sem(name):
            return ctx.enter_context(nc.semaphore(name))

        x_sb = sb("x_sb", [P, NT, D])
        mod = sb("mod", [P, B, 6, D])
        ident = sb("ident", [P, P])
        gate_w = sb("gate_w", [P, E])
        gate_b = sb("gate_b", [P, E])
        w_raw = [sb(f"w_raw{i}", [P, WCOL]) for i in range(2)]
        w_hi = [sb(f"w_hi{i}", [P, WCOL], F32R) for i in range(2)]
        w_lo = [sb(f"w_lo{i}", [P, WCOL], F32R) for i in range(2)]
        stats = sb("stats", [P, 10, 6])
        mv = sb("mv", [P, 10, 2])
        var_eps = sb("var_eps", [P, 10])
        rstd = sb("rstd", [P, 10])
        unused = sb("unused", [P, P])
        unused_pool = sb("unused_pool", [P, 1])
        minus_half = sb("minus_half", [P, 4])
        h2_hi = sb("h2_hi", [P, T], F32R)
        h2_lo = sb("h2_lo", [P, T], F32R)
        comb_s = sb("comb_s", [P, T], F32R)
        h2_now = sb("h2_now", [P, 2, D])
        h2t_now = sb("h2t_now", [P, SEQ])
        scores_of = [sb(f"scores{i}", [P, 2, E + 8]) for i in range(2)]
        chosen = sb("chosen", [P, 2, E + 8])
        grp = sb("grp", [P, 2, 2 * G])
        grp_chosen = sb("grp_chosen", [P, 2, 2 * G])
        grp_top = sb("grp_top", [P, 2, 8])
        grp_mask = sb("grp_mask", [P, 2, G])
        exp_top = sb("exp_top", [P, 2, 8])
        comb = sb("comb", [P, 2, E])
        comb_sum = sb("comb_sum", [P, 2])
        comb_inv = sb("comb_inv", [P, 2])
        comb_of = [sb(f"comb_of{i}", [P, 2, 2 * E]) for i in range(2)]
        combt_of = [sb(f"combt_of{i}", [P, SEQ]) for i in range(2)]

        with attn_mem:
            def asb(name, shape, dt=F32, where=attn_mem):
                return sb(name, shape, dt, where)
            cq = asb("cq", [P, T], F32R)
            ckv = asb("ckv", [P, T], F32R)
            ckv_tok = asb("ckv_tok", [P, NT, DL])
            w_up_hi = asb("w_up_hi", [P, 2, H * DH], F32R)
            w_up_lo = asb("w_up_lo", [P, 2, H * DH], F32R)
            w_vo = asb("w_vo", [P, NP, D])
            h0 = asb("h0", [P, NT, D])
            hT = asb("hT", [P, CH])
            hn = asb("hn", [P, 4, D])
            rope = asb("rope", [P, 2, SEQ])
            w_down = asb("w_down", [P, 2, 2 * DL])
            ln_col = asb("ln_col", [P, 2])
            wv_diag = asb("wv_diag", [P, NP, P])
            wo_t = asb("wo_t", [P, NP, D])
            gate_sign = asb("gate_sign", [P, B, D])
            gate_size = asb("gate_size", [P, B, D])
            with ahead_mem:
                w_up = asb("w_up", [P, 2, H * DH], where=ahead_mem)
                c_t = asb("c_t", [P, B], where=ahead_mem)
                c_rep = asb("c_rep", [P, B, P], where=ahead_mem)
                w_mod = asb("w_mod", [P, 6 * D], where=ahead_mem)
            scaled = [asb(f"scaled{i}", [P, CH]) for i in range(2)]
            swapped = [asb(f"swapped{i}", [P, CH]) for i in range(2)]
            qk = [asb(f"qk{i}", [P, CH]) for i in range(4)]
            row_max = [asb(f"row_max{i}", [P, 4]) for i in range(2)]
            neg_max = [asb(f"neg_max{i}", [P, 4]) for i in range(2)]
            row_sum = [asb(f"row_sum{i}", [P, 4]) for i in range(2)]
            inv_sum = [asb(f"inv_sum{i}", [P, 4]) for i in range(2)]
            probs = [asb(f"probs{i}", [P, 4, SEQ]) for i in range(2)]
            probs_t = [asb(f"probs_t{i}", [P, 2, CH]) for i in range(2)]
            kv_now = asb("kv_now", [P, 2, DL])
            mix_t = [asb(f"mix_t{i}", [P, SEQ]) for i in range(2)]
            att_y = asb("att_y", [P, 2, D])
        with moe_mem:
            def msb(name, shape, dt=F32):
                return sb(name, shape, dt, moe_mem)
            silu_g = [msb(f"silu_g{i}", [P, CH]) for i in range(4)]
            h_u = [msb(f"h_u{i}", [P, CH]) for i in range(4)]
            h_e = [msb(f"h_e{i}", [P, CH]) for i in range(4)]
            h_hi = [msb(f"h_hi{i}", [P, CH], F32R) for i in range(4)]
            h_lo = [msb(f"h_lo{i}", [P, CH], F32R) for i in range(4)]
            y_t = [msb(f"y_t{i}", [P, CH]) for i in range(2)]
            y = [msb(f"y{i}", [P, 4, D]) for i in range(NCH)]

        ps = ctx.enter_context(nc.psum_tensor("ps", [P, 8, CH], F32))
        hT_ps, tok_ps = ps[:, 2, :], ps[:, 5, :]
        rows_ps = [ps[:, i, :] for i in (4, 5, 6, 7, 0, 1, 6, 7)]
        lat_ps = [ps[:, 3 + i, :] for i in range(2)]
        up_ps = [ps[:, i, :] for i in range(2)]
        s_ps = ps[:, 2:4, :].rearrange("p h (c k) -> p (h c) k", c=2)
        t_ps = [ps[:, 4 + i, :] for i in range(2)]
        o_ps = ps[:, 6, :]
        f_ps = ps[:, 7, 0:2 * D]
        side_ps = ps[:, 6, SEQ:2 * SEQ]
        acc = [ps[:, 4 + i, :] for i in range(4)]

        def ring(u, c, r):
            return ps[:, (3 * c + r) % 4, :]

        in_names = ("x", "c_t", "w_mod", "w_down", "w_up", "wv_diag", "wo_t", "ln_col", "rope",
                    "ident", "gate_w", "gate_b")
        in_x = [sem(f"in_x{c}") for c in range(NCH)]
        in_s = {n: sem("in_" + n) for n in in_names[1:]}
        in_w = [sem("in_w_even"), sem("in_w_odd")]
        (c_silu, c_spread, mod_mm, mod_copied, mod_one, w_up_split_hi, w_up_split,
         wvo_mm, wvo_ready) = map(sem, (
            "c_silu", "c_spread", "mod_mm", "mod_copied", "mod_one", "w_up_split_hi", "w_up_split",
            "wvo_mm", "wvo_ready"))
        st_a, ag_a, nm_a, ml_a, h0_ready, st_b, ag_b, hn_ready, hT_mm, hT_ready, \
            lat_mm, cq_hi, ckv_hi, ckvt_ready, cq_ready, ckv_ready = map(sem, (
                "st_a", "ag_a", "nm_a", "ml_a", "h0_ready", "st_b", "ag_b", "hn_ready",
                "hT_mm", "hT_ready", "lat_mm", "cq_hi", "ckv_hi", "ckvt_ready", "cq_ready", "ckv_ready"))
        up_mm, scaled_ready, swap_ready, sin_done, qk_ready, s_mm, max_ready, neg_ready, exp_done, \
            inv_ready, probs0_ready, probs0b_ready, probs1_ready, t_mm, t0_copied, t1_copied, kv_ready, pv_mm, mix_ready, fin_mm, \
            fin_copied, gated, x2_ready = map(sem, (
                "up_mm", "scaled_ready", "swap_ready", "sin_done", "qk_ready", "s_mm", "max_ready",
                "neg_ready", "exp_done", "inv_ready", "probs0_ready", "probs0b_ready", "probs1_ready", "t_mm", "t0_copied", "t1_copied",
                "kv_ready", "pv_mm", "mix_ready", "fin_mm", "fin_copied", "gated", "x2_ready"))
        rs_a, rs_b, rs_c = ([sem(f"var_{k}"), sem(f"rstd_{k}")] for k in "abc")
        half_ready, sign_ready, size_ready, gate_ready = map(sem, (
            "half_ready", "sign_ready", "size_ready", "gate_ready"))
        st_c, ag_c, nm_c, ml_c, h2_ready, h2t_mm, h2t_ready, h2hi_ready, h2lo_ready = map(sem, (
            "st_c", "ag_c", "nm_c", "ml_c", "h2_ready", "h2t_mm", "h2t_ready", "h2hi_ready",
            "h2lo_ready"))
        filler_ready, logit_mm, exp_ready, plus_ready, sig_ready, sc_ready, gm_ready, gtop, gtop_set, \
            gpick, gmask_ready, masked_ready, etop, etop_set, epick, comb_ready, csum_ready, ceps, \
            cinv, comb2_ready, combt_mm, combt_ready, comb_hi, combs_ready = map(sem, (
                "filler_ready", "logit_mm", "exp_ready", "plus_ready", "sig_ready", "sc_ready",
                "gm_ready", "gtop", "gtop_set", "gpick", "gmask_ready", "masked_ready", "etop",
                "etop_set", "epick", "comb_ready", "csum_ready", "ceps", "cinv", "comb2_ready",
                "combt_mm", "combt_ready", "comb_hi", "combs_ready"))
        w_rounded, w_split, w_split_down, gate_mm, upx_mm, sel_mm, silu_ready, hu_ready, he_ready, \
            hhi_ready, hlo_ready, down_mm = map(sem, (
                "w_rounded", "w_split", "w_split_down", "gate_mm", "upx_mm", "sel_mm",
                "silu_ready", "hu_ready", "he_ready", "hhi_ready", "hlo_ready", "down_mm"))
        yt_ready, y_mm, y_gated, y_ready, y_ready_pool, stored = map(sem, (
            "yt_ready", "y_mm", "y_gated", "y_ready", "y_ready_pool", "stored"))

        block = ctx.enter_context(nc.Block())

        @block.sync
        def _(sp):
            sp.dma_start(c_t[:, :], io["c_t"]).then_inc(in_s["c_t"], 16)
            sp.dma_start(w_mod[:, :], io["w_mod"]).then_inc(in_s["w_mod"], 16)
            xv = io["x"].rearrange("(c t p) d -> c p t d", c=NCH, p=P)
            for c in range(NCH):
                sp.dma_start(x_sb[:, 4 * c:4 * c + 4, :], xv[c]).then_inc(in_x[c], 16)
            for name, tile in (("ident", ident), ("ln_col", ln_col), ("w_down", w_down), ("w_up", w_up),
                               ("rope", rope), ("wv_diag", wv_diag), ("wo_t", wo_t),
                               ("gate_w", gate_w)):
                t = tile[(slice(None),) * len(tile.shape)]
                sp.dma_start(t, io[name]).then_inc(in_s[name], 16)
            sp.dma_start(gate_b[:, :], io["gate_b"].to_broadcast([P, E])).then_inc(in_s["gate_b"], 16)
            for p, par, _ in pairs(sp):
                wait(sp, w_split_down, p - 1)
                sp.dma_start(w_raw[par][:, :], io["w_pairs"][ds(p, 1)].rearrange("o p n -> (o p) n")
                             ).then_inc(in_w[par], 16)
            ov = out.rearrange("(c t p) d -> c p t d", c=NCH, p=P)
            for c in range(NCH):
                if c == 2:
                    sp.wait_ge(y_ready_pool, 1)
                else:
                    sp.wait_ge(y_ready, min(c, 2) + 1)
                sp.dma_start(ov[c], y[c][:, :, :]).then_inc(stored, 16)
            sp.wait_ge(stored, 16 * NCH)

        @block.tensor
        def _(pe):
            pe.wait_ge(c_spread, 1)
            pe.wait_ge(in_s["w_mod"], 16)
            for b in range(B):
                mm = pe.matmul(ps[:, b // 2, (b % 2) * 2 * D:(b % 2 + 1) * 2 * D], c_rep[:, b, :],
                               w_mod[:, 0:2 * D], start=True, stop=True)
                if b % 2:
                    mm.then_inc(mod_mm, 1)
            def other_rows(batches):
                for b in batches:
                    if b >= 6:
                        pe.wait_ge(mod_copied, b + 1)
                    pe.matmul(rows_ps[b], c_rep[:, b, :], w_mod[:, 2 * D:6 * D], start=True,
                              stop=True).then_inc(mod_mm, 1)

            other_rows(range(4))
            pe.wait_ge(in_s["ident"], 16)
            pe.wait_ge(in_s["w_down"], 16)
            pe.wait_ge(mod_copied, B // 2)

            def project(n, b, j):
                wait(pe, swap_ready, n - 1)
                for half, lat in ((0, cq), (1, ckv)):
                    for w in (w_up_hi, w_up_lo):
                        mm = pe.matmul(up_ps[j % 2][:, half * SEQ:(half + 1) * SEQ],
                                       w[:, half, j * P:(j + 1) * P], lat[:, ds(b * SEQ, SEQ)],
                                       start=(w is w_up_hi), stop=(w is w_up_lo))
                mm.then_inc(up_mm, 1)

            for c in chunks(pe):
                pe.wait_ge(hn_ready, 4 * c + 4)
                for k in range(4):
                    mm = pe.transpose(hT_ps[:, k * P:(k + 1) * P], hn[:, k, :], ident[:, :])
                mm.then_inc(hT_mm, 1)
                if isinstance(c, int) and c == NCH - 1:
                    pe.wait_ge(w_up_split, 4)
                    for n in range(3):
                        project(n, 0, n)
                pe.wait_ge(hT_ready, c + 1)
                if isinstance(c, int) and c == 0:
                    pe.wait_ge(mod_copied, B // 2 + 2)
                wait(pe, cq_ready, c)
                wait(pe, ckv_ready, c)
                wait(pe, ckvt_ready, c)
                pe.matmul(lat_ps[0], w_down[:, 0, :], hT[:, :], start=True, stop=True)
                pe.matmul(lat_ps[1], w_down[:, 1, :], hT[:, :], start=True, stop=True)
                for k in range(4):
                    mm = pe.matmul(tok_ps[:, k * DL:(k + 1) * DL], hT[:, k * P:(k + 1) * P],
                                   w_down[:, 1, 0:DL], start=True, stop=True)
                mm.then_inc(lat_mm, 1)
                if isinstance(c, int) and c == 0:
                    other_rows(range(4, B))
                if isinstance(c, int) and c == NCH - 1:
                    pe.wait_ge(in_s["wv_diag"], 16)
                    pe.wait_ge(in_s["wo_t"], 16)
                    pe.wait_ge(mod_copied, B // 2 + B)
                    for j in range(NP):
                        mm = pe.matmul(ps[:, 6 + j // 4, (j % 4) * D:(j % 4 + 1) * D],
                                       wv_diag[:, j, :], wo_t[:, j, :], start=True, stop=True)
                    mm.then_inc(wvo_mm, 1)
            pe.wait_ge(cq_ready, NCH)
            pe.wait_ge(ckv_ready, NCH)
            pe.wait_ge(ckvt_ready, NCH)

            def score(n, b, j):
                pe.wait_ge(qk_ready, n + 1)
                for h in range(2):
                    wait(pe, exp_done, 4 * n - 2 + 2 * h)
                    r = slice(DH * h, DH * (h + 1))
                    for qh in range(2):
                        mm = pe.matmul(s_ps[:, 2 * h + qh, :], qk[j % 4][r, qh * P:(qh + 1) * P],
                                       qk[j % 4][r, SEQ:2 * SEQ], start=True, stop=True)
                    mm.then_inc(s_mm, 1)

            def turn(n, b, j):
                for h in range(2):
                    wait(pe, (t0_copied, t1_copied)[h], n)
                    if h == 1:
                        pe.wait_ge(probs1_ready, n + 1)
                    for qh in range(2):
                        if h == 0:
                            pe.wait_ge((probs0_ready, probs0b_ready)[qh], n + 1)
                        for kh in range(2):
                            at = kh * SEQ + qh * P
                            mm = pe.transpose(t_ps[h][:, at:at + P],
                                              probs[j % 2][:, 2 * h + qh, kh * P:(kh + 1) * P], ident[:, :])
                    mm.then_inc(t_mm, 1)

            def mix(n, b, j):
                pe.wait_ge(t0_copied, n + 1)
                pe.wait_ge(t1_copied, n + 1)
                pe.wait_ge(kv_ready, b + 1)
                wait(pe, mix_ready, n)
                for kh in range(2):
                    for h in range(2):
                        mm = pe.matmul(o_ps[DL * h:DL * (h + 1), 0:SEQ], kv_now[:, kh, :],
                                       probs_t[j % 2][:, h, kh * SEQ:(kh + 1) * SEQ],
                                       start=(kh == 0), stop=(kh == 1))
                mm.then_inc(pv_mm, 1)

            def finish(n, b, j):
                pe.wait_ge(mix_ready, n + 1)
                if isinstance(b, int) and b == 0 and j == 0:
                    pe.wait_ge(wvo_ready, 1)
                if j == 0:
                    wait(pe, fin_copied, b)
                for qh in range(2):
                    mm = pe.matmul(f_ps[:, qh * D:(qh + 1) * D], mix_t[j % 2][:, qh * P:(qh + 1) * P],
                                   w_vo[:, j, :], start=(j == 0 and qh == 0), stop=(j == NP - 1),
                                   skip_group_check=True)
                mm.then_inc(fin_mm, 1)

            def h2_turn(b):
                pe.wait_ge(h2_ready, b + 1)
                for k in range(2):
                    mm = pe.transpose(side_ps[:, k * P:(k + 1) * P], h2_now[:, k, :], ident[:, :])
                mm.then_inc(h2t_mm, 1)

            def route(b):
                pe.wait_ge(h2t_ready, b + 1)
                for k in range(2):
                    mm = pe.matmul(side_ps[:, k * E:(k + 1) * E], h2t_now[:, k * P:(k + 1) * P],
                                   gate_w[:, :], start=True, stop=True)
                mm.then_inc(logit_mm, 1)

            def comb_turn(b, to):
                pe.wait_ge(comb2_ready, b + 1)
                for k in range(2):
                    mm = pe.transpose(to[:, k * P:(k + 1) * P], comb_of[last(b)][:, k, :], ident[:, :])
                mm.then_inc(combt_mm, 1)

            score(0, 0, 0)
            pe.wait_ge(in_s["gate_w"], 16)
            for n, b, j in steps(pe):
                side = None
                if j == 0 and behind(b, 2):
                    pe.wait_ge(mix_ready, n - 1)
                    route(b - 2)
                    side = (exp_ready, b - 1)
                elif j == 6 and behind(b, 2):
                    pe.wait_ge(mix_ready, n - 1)
                    comb_turn(b - 2, side_ps)
                    side = (combt_ready, b - 1)
                elif j == 7 and behind(b, 1):
                    pe.wait_ge(mix_ready, n - 1)
                    h2_turn(b - 1)
                    side = (h2t_ready, b)
                for stage, by in ((score, 1), (mix, -1), (finish, -2), (project, 3), (turn, 0)):
                    at = later(b, j, by)
                    if stage is mix and side:
                        pe.wait_ge(*side)
                    if at:
                        stage(n + by, *at)
            mix(B * NP - 1, B - 1, NP - 1)
            finish(B * NP - 2, B - 1, NP - 2)
            finish(B * NP - 1, B - 1, NP - 1)
            route(B - 2)

            def product(bank, par, cols, c):
                for a, x, k in ((w_hi, h2_hi, 0), (w_hi, h2_lo, 1), (w_lo, h2_hi, 2)):
                    mm = pe.matmul(bank, a[par][:, cols], x[:, c * CH:(c + 1) * CH],
                                   start=(k == 0), stop=(k == 2))
                return mm

            def down(u, c, par, first, last):
                pe.wait_ge(hlo_ready, u + 1)
                wcols = slice(256, 384)
                for a, x, k in ((w_hi, h_hi, 0), (w_hi, h_lo, 1), (w_lo, h_hi, 2)):
                    mm = pe.matmul(acc[c], a[par][:, wcols], x[c][:, :], start=(first and k == 0),
                                   stop=(last and k == 2), skip_group_check=True)
                mm.then_inc(down_mm, 1)

            for p, par, _ in pairs(pe):
                shared = isinstance(p, int) and p == 0
                pe.wait_ge(w_split, p + 1)
                for c in range(NCH):
                    u = p * NCH + c
                    wait(pe, he_ready, u - 1)
                    if shared:
                        pe.wait_ge(h2lo_ready, 2 * c + 2)
                    product(ring(u, c, 0), par, slice(0, 128), c).then_inc(gate_mm, 1)
                    wait(pe, silu_ready, u)
                    product(ring(u, c, 1), par, slice(128, 256), c).then_inc(upx_mm, 1)
                    if not shared:
                        wait(pe, hu_ready, u)
                        if isinstance(p, int) and p == 1:
                            pe.wait_ge(combs_ready, 2 * c + 2)
                        pe.matmul(ring(u, c, 2), w_hi[par][:, 384:512], comb_s[:, c * CH:(c + 1) * CH],
                                  start=True, stop=True).then_inc(sel_mm, 1)
                    if shared and c == 1:
                        pe.wait_ge(exp_ready, B - 1)
                        h2_turn(B - 1)
                    if shared and c == 2:
                        route(B - 1)
                    if shared and c < 2:
                        continue
                    if isinstance(p, int) and p == 1:
                        if c == 0:
                            pe.wait_ge(exp_ready, B)
                        elif c == 1:
                            comb_turn(B - 2, ps[:, 7, 0:SEQ])
                            continue
                        elif c == 2:
                            pe.wait_ge(combt_ready, B - 1)
                            comb_turn(B - 1, ps[:, 7, SEQ:2 * SEQ])
                            pe.wait_ge(combt_ready, B)
                            down(u - 3, 3, 0, True, False)
                    if shared and c == 2:
                        pe.wait_ge(t1_copied, B * NP)
                    if c == 2:
                        pe.wait_ge(w_split_down, p + 1)
                    down(u - 2, (c - 2) % 4, par if c >= 2 else 1 - par,
                         isinstance(p, int) and u - 2 < NCH, False)
            U = NPAIR * NCH
            for c in range(NCH):
                if c < 2:
                    down(U - 2 + c, 2 + c, 0, False, True)
                pe.wait_ge(yt_ready, c + 1)
                for k in range(4):
                    mm = pe.transpose(ps[:, c, k * P:(k + 1) * P], y_t[c % 2][:, k * P:(k + 1) * P],
                                      ident[:, :])
                mm.then_inc(y_mm, 1)

        @block.vector
        def _(dve):
            word = count()

            def wait_by_memset(sem, value):
                dve.wait_ge(sem, value)
                at = next(word) % P
                return dve.memset(unused[:, at:at + 1], 0.0)

            def layernorm_stats(src, k0, st, ag, rs, done, tiles=4):
                for k in range(tiles):
                    dve.bn_stats(stats[:, k0 + k, :], src(k)).then_inc(st, 1)
                wait_by_memset(st, tiles * done + tiles)
                for k in range(tiles):
                    dve.bn_aggr(mv[:, k0 + k, :], stats[:, k0 + k, :]).then_inc(ag, 1)
                dve.wait_ge(ag, tiles * done + tiles)
                dve.tensor_scalar(var_eps[:, k0:k0 + tiles], mv[:, k0:k0 + tiles, 1], LN_EPS, None,
                                  ALU.add).then_inc(rs[0], 1)

            def normalise(dst, src, k0, rs, done, ready, tiles=4):
                dve.wait_ge(rs[1], done + 1)
                for k in range(tiles):
                    dve.tensor_scalar(dst(k), src(k), mv[:, k0 + k, 0:1], rstd[:, k0 + k:k0 + k + 1],
                                      ALU.subtract, ALU.mult).then_inc(ready, 1)

            dve.wait_ge(c_silu, 1)
            dve.tensor_copy(c_rep[:, :, :], c_t[:, :].unsqueeze(2).to_broadcast([P, B, P])
                            ).then_inc(c_spread, 1)

            def one_more(batches, row, copied):
                dve.wait_ge(mod_copied, copied)
                dve.tensor_scalar(mod[:, batches, row, :], mod[:, batches, row, :], 1.0, None, ALU.add
                                  ).then_inc(mod_one, 1)

            def latent_low(c):
                for bank, lat, hi, ready in ((0, cq, cq_hi, cq_ready), (1, ckv, ckv_hi, ckv_ready)):
                    dve.wait_ge(hi, c + 1)
                    dve.tensor_tensor(lat[DL:P, ds(c * CH, CH)], lat_ps[bank][DL:P, :],
                                      lat[DL:P, ds(c * CH, CH)], ALU.subtract).then_inc(ready, 1)

            def x_tile(c, k):
                return x_sb[:, ds(c * 4 + k, 1), :]

            def h0_tile(c, k):
                return h0[:, ds(c * 4 + k, 1), :]

            def stats_a(c):
                layernorm_stats(lambda k: x_tile(c, k), 0, st_a, ag_a, rs_a, c)

            def rotate(n, b, j):
                dve.wait_ge(up_mm, n + 1)
                wait(dve, qk_ready, n - 1)
                dve.tensor_tensor(scaled[j % 2][:, :].rearrange("p (a t) -> p a t", a=2),
                                  up_ps[j % 2].rearrange("p (a t) -> p a t", a=2),
                                  bcast(rope[:, 0, :], 1, 2), ALU.mult).then_inc(scaled_ready, 1)
                dve.stream_shuffle(swapped[j % 2][:, :], up_ps[j % 2], SWAP).then_inc(swap_ready, 1)

            dve.wait_ge(in_x[0], 16)
            stats_a(0)
            for c in chunks(dve):
                normalise(lambda k: h0_tile(c, k), lambda k: x_tile(c, k), 0, rs_a, c, nm_a)
                if isinstance(c, int) and c == 0:
                    one_more(slice(0, 2), 1, 1)
                    dve.wait_ge(mod_one, 1)
                dve.wait_ge(nm_a, 4 * c + 4)
                h0c = h0[:, ds(c * 4, 4), :].rearrange("p (b t) d -> p b t d", t=2)
                dve.tensor_tensor(h0c, h0c, bcast(mod[:, ds(c * 2, 2), 1, :], 2, 2), ALU.mult
                                  ).then_inc(ml_a, 1)
                dve.wait_ge(ml_a, c + 1)
                dve.tensor_tensor(h0c, h0c, bcast(mod[:, ds(c * 2, 2), 0, :], 2, 2), ALU.add
                                  ).then_inc(h0_ready, 1)
                wait_by_memset(h0_ready, c + 1)
                layernorm_stats(lambda k: h0_tile(c, k), 4, st_b, ag_b, rs_b, c)
                if isinstance(c, int) and c == 0:
                    for k in range(1, NCH):
                        dve.wait_ge(in_x[k], 16)
                if not (isinstance(c, int) and c > 0):
                    stats_a(c + 1)
                wait(dve, hT_mm, c)
                normalise(lambda k: hn[:, k:k + 1, :], lambda k: h0_tile(c, k), 4, rs_b, c, hn_ready)
                if isinstance(c, int) and c == 0:
                    one_more(slice(2, B), 1, B // 2)
                    dve.wait_ge(mod_one, 2)
                else:
                    latent_low(c - 1)
            dve.wait_ge(in_s["rope"], 16)
            for n in range(3):
                rotate(n, 0, n)
            latent_low(NCH - 1)

            def gates(j):
                i = j // 3
                a = (2, 5)[i]
                gate = mod[:, :, a, :]
                if j % 3 == 0:
                    dve.wait_ge(mod_copied, B // 2 + B)
                    dve.tensor_scalar(gate_sign[:, :, :], gate, 0.0, 0.5, ALU.is_ge, ALU.subtract
                                      ).then_inc(sign_ready, 1)
                elif j % 3 == 1:
                    dve.wait_ge(sign_ready, i + 1)
                    dve.scalar_tensor_tensor(gate_size[:, :, :], gate, 4.0, gate_sign[:, :, :],
                                             ALU.mult, ALU.mult).then_inc(size_ready, 1)
                else:
                    dve.wait_ge(size_ready, i + 1)
                    dve.scalar_tensor_tensor(gate, gate_size[:, :, :], 0.5, gate_sign[:, :, :],
                                             ALU.max, ALU.mult).then_inc(gate_ready, 1)
                    dve.wait_ge(gate_ready, i + 1)

            def maximum(n, b, j):
                for h in range(2):
                    rows = slice(2 * h, 2 * h + 2)
                    dve.wait_ge(s_mm, 2 * n + h + 1)
                    dve.tensor_reduce(row_max[j % 2][:, rows], s_ps[:, rows, :], AX.X, ALU.max
                                      ).then_inc(max_ready, 1)
                    dve.wait_ge(max_ready, 2 * n + h + 1)
                    dve.tensor_scalar(neg_max[j % 2][:, rows], row_max[j % 2][:, rows], -QK_SCALE, None,
                                      ALU.mult).then_inc(neg_ready, 1)

            def invert(n, b, j):
                dve.wait_ge(exp_done, 4 * n + 4)
                dve.reciprocal(inv_sum[j % 2][:, :], row_sum[j % 2][:, :]).then_inc(inv_ready, 1)
                dve.wait_ge(inv_ready, n + 1)
                dve.tensor_scalar(probs[j % 2][:, 0, :], probs[j % 2][:, 0, :],
                                  inv_sum[j % 2][:, 0:1], None, ALU.mult).then_inc(probs0_ready, 1)

            def output(b):
                dve.wait_ge(fin_mm, NP * b + NP)
                dve.wait_ge(x2_ready, b + 1)
                dve.tensor_tensor(att_y[:, :, :], f_ps.rearrange("p (t d) -> p t d", t=2),
                                  h0[:, ds(b * 2, 2), :], ALU.add).then_inc(fin_copied, 1)

            def h2_stats(b):
                wait_by_memset(x2_ready, b + 2)
                layernorm_stats(lambda k: x_sb[:, ds(2 * b + k, 1), :], 8, st_c, ag_c, rs_c, b, 2)

            def h2_scale(b):
                wait(dve, h2t_mm, b)
                normalise(lambda k: h2_now[:, k:k + 1, :], lambda k: x_sb[:, ds(2 * b + k, 1), :],
                          8, rs_c, b, nm_c, 2)

            def h2_shift(b):
                dve.wait_ge(nm_c, 2 * b + 2)
                dve.tensor_tensor(h2_now[:, :, :], h2_now[:, :, :],
                                  mod[:, ds(b, 1), 4, :].to_broadcast([P, 2, D]), ALU.mult
                                  ).then_inc(ml_c, 1)
                dve.wait_ge(ml_c, b + 1)
                dve.tensor_tensor(h2_now[:, :, :], h2_now[:, :, :],
                                  mod[:, ds(b, 1), 3, :].to_broadcast([P, 2, D]), ALU.add
                                  ).then_inc(h2_ready, 1)

            def all_scores(b):
                return scores_of[last(b)][:, :, 0:E]

            def by_group(b):
                return all_scores(b).rearrange("p t (g e) -> p t g e", g=G)

            def sigmoid(b):
                sc = all_scores(b)
                dve.wait_ge(exp_ready, b + 1)
                dve.tensor_scalar(sc, sc, 1.0, None, ALU.add).then_inc(plus_ready, 1)
                dve.wait_ge(plus_ready, b + 1)
                dve.reciprocal(sc, sc).then_inc(sig_ready, 1)

            def group_scores(b):
                sc = all_scores(b)
                dve.wait_ge(sig_ready, b + 1)
                dve.tensor_tensor(sc, sc, bcast(gate_b[:, :], 1, 2), ALU.add).then_inc(sc_ready, 1)
                dve.wait_ge(sc_ready, b + 1)
                dve.tensor_reduce(grp[:, :, 0:G], by_group(b), AX.X, ALU.max).then_inc(gm_ready, 1)

            def take(picked, top, of, n, keep, found, cleared, taken, b):
                for k in range(2):
                    dve.max(top[:, k, :], of[:, k, 0:n]).then_inc(found, 1)
                dve.wait_ge(found, 2 * b + 2)
                dve.memset(top[:, :, keep:8], FILLER).then_inc(cleared, 1)
                wait_by_memset(cleared, b + 1)
                for k in range(2):
                    dve.match_replace(picked[:, k, :], top[:, k, :], of[:, k, :], TAKEN
                                      ).then_inc(taken, 1)

            def choose_groups(b):
                wait_by_memset(gm_ready, b + 1)
                take(grp_chosen, grp_top, grp, G, K_GRP, gtop, gtop_set, gpick, b)

            def mask_groups(b):
                dve.wait_ge(gpick, 2 * b + 2)
                dve.tensor_scalar(grp_mask[:, :, :], grp_chosen[:, :, 0:G], TAKEN, None, ALU.is_equal
                                  ).then_inc(gmask_ready, 1)
                dve.wait_ge(gmask_ready, b + 1)
                dve.tensor_tensor(by_group(b), by_group(b),
                                  grp_mask[:, :, :].unsqueeze(3).to_broadcast([P, 2, G, E // G]),
                                  ALU.mult).then_inc(masked_ready, 1)

            def choose_experts(b):
                wait_by_memset(masked_ready, b + 1)
                take(chosen, exp_top, scores_of[last(b)], E, K_EXP, etop, etop_set, epick, b)

            def weights_sum(b):
                dve.wait_ge(epick, 2 * b + 2)
                dve.scalar_tensor_tensor(comb[:, :, :], chosen[:, :, 0:E], TAKEN, all_scores(b), ALU.is_equal,
                                         ALU.mult).then_inc(comb_ready, 1)
                dve.wait_ge(comb_ready, b + 1)
                dve.tensor_reduce(comb_sum[:, :], comb[:, :, :], AX.X, ALU.add).then_inc(csum_ready, 1)
                dve.wait_ge(csum_ready, b + 1)
                dve.tensor_scalar(comb_sum[:, :], comb_sum[:, :], 1e-8, None, ALU.add).then_inc(ceps, 1)
                dve.wait_ge(ceps, b + 1)
                dve.reciprocal(comb_inv[:, :], comb_sum[:, :]).then_inc(cinv, 1)

            def expert_weights(b):
                dve.wait_ge(cinv, b + 1)
                if not last(b):
                    wait(dve, combt_mm, b)
                for half in range(2):
                    ins = dve.tensor_tensor(comb_of[last(b)][:, :, half * E:(half + 1) * E], comb[:, :, :],
                                            comb_inv[:, :].unsqueeze(2).to_broadcast([P, 2, E]),
                                            ALU.mult)
                ins.then_inc(comb2_ready, 1)

            def comb_low(b):
                dve.wait_ge(comb_hi, b + 1)
                cs = comb_s[E:P, ds(b * SEQ, SEQ)]
                dve.tensor_tensor(cs, combt_of[last(b)][E:P, :], cs, ALU.subtract).then_inc(combs_ready, 1)

            maximum(0, 0, 0)
            invert(0, 0, 0)
            dve.wait_ge(in_s["gate_b"], 16)
            dve.wait_ge(filler_ready, 3)
            for n, b, j in steps(dve):
                if later(b, j, 1):
                    maximum(n + 1, *later(b, j, 1))
                if isinstance(b, int) and b == 0:
                    if j < 6:
                        gates(j)
                    elif j == 6:
                        one_more(slice(0, B), 4, B // 2 + B)
                        dve.wait_ge(mod_one, 3)
                    else:
                        dve.wait_ge(in_w[0], 16)
                        dve.tensor_copy(w_hi[0][:, :], w_raw[0][:, :]).then_inc(w_rounded, 1)
                for stage, when, by in ((sigmoid, 0, 2), (group_scores, 1, 2), (choose_groups, 1, 2),
                                        (mask_groups, 2, 2), (choose_experts, 2, 2), (h2_stats, 3, 1),
                                        (weights_sum, 4, 2), (expert_weights, 5, 2),
                                        (h2_scale, 5, 1), (h2_shift, 6, 1), (comb_low, 7, 2)):
                    if j == when and behind(b, by):
                        stage(b - by)
                for stage, by in ((invert, 1), (rotate, 3)):
                    if later(b, j, by):
                        stage(n + by, *later(b, j, by))
                if j == 1 and behind(b, 1):
                    output(b - 1)
            output(B - 1)
            sigmoid(B - 2)
            h2_stats(B - 1)

            def round_weights(par, value):
                dve.wait_ge(in_w[par], value)
                dve.tensor_copy(w_hi[par][:, :], w_raw[par][:, :]).then_inc(w_rounded, 1)

            for p, par, loads in pairs(dve):
                for c in range(NCH):
                    u = p * NCH + c
                    if c == (3 if isinstance(p, int) and p == 1 else 2) and loads is not None:
                        wait(dve, down_mm, NCH * p)
                        round_weights(1 - par, 16 * loads)
                    dve.wait_ge(upx_mm, u + 1)
                    dve.wait_ge(silu_ready, u + 1)
                    shared = isinstance(p, int) and p == 0
                    dve.tensor_tensor((h_e if shared else h_u)[c][:, :], ring(u, c, 1),
                                      silu_g[c][:, :], ALU.mult).then_inc(hu_ready, 1)
                    for stage, when, b in ((comb_low, 6, 6),):
                        if isinstance(u, int) and u == when:
                            stage(b)
                    if shared:
                        wait_by_memset(hu_ready, u + 1).then_inc(he_ready, 1)
                    else:
                        dve.wait_ge(sel_mm, u + 1 - NCH)
                        dve.wait_ge(hu_ready, u + 1)
                        wait(dve, hlo_ready, u - 3)
                        dve.tensor_tensor(h_e[c][:, :], ring(u, c, 2), h_u[c][:, :], ALU.mult
                                          ).then_inc(he_ready, 1)
                    for stage, when, b in ((h2_scale, 0, 7), (h2_shift, 0, 7),
                                           (group_scores, 1, 6), (choose_groups, 1, 6),
                                           (mask_groups, 1, 6), (choose_experts, 2, 6),
                                           (sigmoid, 2, 7), (group_scores, 2, 7), (weights_sum, 3, 6),
                                           (expert_weights, 3, 6), (choose_groups, 3, 7),
                                           (mask_groups, 4, 7), (choose_experts, 4, 7),
                                           (weights_sum, 5, 7), (expert_weights, 5, 7),
                                           (comb_low, 6, 7)):
                        if isinstance(u, int) and u == when:
                            stage(b)
            for c in range(NCH):
                dve.wait_ge(y_mm, c + 1)
                dve.tensor_tensor(y[c][:, :, :].rearrange("p (b t) d -> p b t d", t=2),
                                  ps[:, c, :].rearrange("p (b t d) -> p b t d", t=2, d=D),
                                  bcast(mod[:, 2 * c:2 * c + 2, 5, :], 2, 2), ALU.mult
                                  ).then_inc(y_gated, 1)
                if c == 2:
                    continue
                dve.wait_ge(y_gated, c + 1)
                dve.tensor_tensor(y[c][:, :, :], y[c][:, :, :], x_sb[:, 4 * c:4 * c + 4, :],
                                  ALU.add).then_inc(y_ready, 1)

        @block.scalar
        def _(act):
            act.wait_ge(in_s["c_t"], 16)
            act.activation(c_t[:, :], c_t[:, :], ACT.Silu).then_inc(c_silu, 1)
            for k in range(B // 2):
                act.wait_ge(mod_mm, k + 1)
                act.copy(mod[:, 2 * k:2 * k + 2, 0:2, :].rearrange("p b a d -> p b (a d)"),
                         ps[:, k, :].rearrange("p (b d) -> p b d", b=2)).then_inc(mod_copied, 1)

            def other_rows(batches):
                for b in batches:
                    act.wait_ge(mod_mm, B // 2 + b + 1)
                    act.copy(mod[:, b, 2:6, :].rearrange("p a d -> p (a d)"), rows_ps[b]
                             ).then_inc(mod_copied, 1)

            act.wait_ge(in_s["w_up"], 16)
            act.copy(w_up_hi[:, :, :], w_up[:, :, :]).then_inc(w_up_split_hi, 1)
            other_rows(range(4))
            act.wait_ge(in_s["ln_col"], 16)
            for c in chunks(act):
                act.wait_ge(hT_mm, c + 1)
                wait(act, lat_mm, c)
                act.activation(hT[:, :], hT_ps, ACT.Identity, bias=ln_col[:, 1:2],
                               scale=ln_col[:, 0:1]).then_inc(hT_ready, 1)
                act.wait_ge(lat_mm, c + 1)
                act.copy(cq[:, ds(c * CH, CH)], lat_ps[0]).then_inc(cq_hi, 1)
                act.copy(ckv[:, ds(c * CH, CH)], lat_ps[1]).then_inc(ckv_hi, 1)
                act.copy(ckv_tok[:, ds(c * 4, 4), :], tok_ps[:, 0:4 * DL].rearrange(
                    "p (t d) -> p t d", t=4)).then_inc(ckvt_ready, 1)
                if isinstance(c, int) and c == 0:
                    other_rows(range(4, B))
                if isinstance(c, int) and c == NCH - 1:
                    act.wait_ge(wvo_mm, 1)
                    act.copy(w_vo[:, :, :], ps[:, 6:8, :].rearrange("p a (b d) -> p (a b) d", d=D)
                             ).then_inc(wvo_ready, 1)

            def exponent(n, b, j):
                wait(act, t_mm, 2 * (n - 1))
                wait(act, inv_ready, n - 1)
                for i in range(4):
                    if i % 2 == 0:
                        act.wait_ge(neg_ready, 2 * n + i // 2 + 1)
                    act.activation(probs[j % 2][:, i, :], s_ps[:, i, :], ACT.Exp,
                                   bias=neg_max[j % 2][:, i:i + 1], scale=QK_SCALE,
                                   accum_out=row_sum[j % 2][:, i:i + 1]).then_inc(exp_done, 1)

            def normalise(n, b, j):
                act.wait_ge(inv_ready, n + 1)
                act.activation(probs[j % 2][:, 1, :], probs[j % 2][:, 1, :], ACT.Copy,
                               scale=inv_sum[j % 2][:, 1:2]).then_inc(probs0b_ready, 1)

            def copy_turned(n, b, j):
                wait(act, pv_mm, n - 1)
                for h in range(2):
                    act.wait_ge(t_mm, 2 * n + 1 + h)
                    act.copy(probs_t[j % 2][:, h, :], t_ps[h]).then_inc((t0_copied, t1_copied)[h], 1)

            def copy_mix(n, b, j):
                act.wait_ge(pv_mm, n + 1)
                wait(act, fin_mm, n - 1)
                act.copy(mix_t[j % 2][:, :], o_ps[:, 0:SEQ]).then_inc(mix_ready, 1)

            def copy_h2t(b):
                act.wait_ge(h2t_mm, b + 1)
                wait(act, logit_mm, b)
                wait(act, h2lo_ready, b)
                act.copy(h2t_now[:, :], side_ps).then_inc(h2t_ready, 1)

            def h2_high(b):
                act.wait_ge(h2t_ready, b + 1)
                act.copy(h2_hi[:, ds(b * SEQ, SEQ)], h2t_now[:, :]).then_inc(h2hi_ready, 1)

            def logit_exp(b):
                act.wait_ge(logit_mm, b + 1)
                if not last(b):
                    wait(act, comb2_ready, b)
                act.activation(scores_of[last(b)][:, :, 0:E], side_ps[:, 0:2 * E].rearrange("p (t e) -> p t e", e=E),
                               ACT.Exp, scale=-1.0).then_inc(exp_ready, 1)

            def latents_now(n, b):
                wait(act, pv_mm, n)
                act.copy(kv_now[:, :, :], ckv_tok[:, ds(b * 2, 2), :]).then_inc(kv_ready, 1)

            def copy_combt(b, of):
                act.wait_ge(combt_mm, b + 1)
                if not last(b):
                    wait(act, combs_ready, b)
                act.copy(combt_of[last(b)][:, :], of).then_inc(combt_ready, 1)

            def comb_high(b):
                act.wait_ge(combt_ready, b + 1)
                act.copy(comb_s[:, ds(b * SEQ, SEQ)], combt_of[last(b)][:, :]).then_inc(comb_hi, 1)

            exponent(0, 0, 0)
            normalise(0, 0, 0)
            for n, b, j in steps(act):
                if j == 0 and behind(b, 2):
                    logit_exp(b - 2)
                elif j == 6 and behind(b, 2):
                    copy_combt(b - 2, side_ps)
                elif j == 7 and behind(b, 1):
                    copy_h2t(b - 1)
                for stage, by in ((copy_turned, -1), (exponent, 1), (copy_mix, -1), (normalise, 1)):
                    at = later(b, j, by)
                    if at:
                        stage(n + by, *at)
                if j == 0:
                    latents_now(n, b)
                elif j == 6 and behind(b, 2):
                    comb_high(b - 2)
                elif j == 7 and behind(b, 1):
                    h2_high(b - 1)
            copy_turned(B * NP - 1, B - 1, NP - 1)
            copy_mix(B * NP - 1, B - 1, NP - 1)
            logit_exp(B - 2)

            def silu(u, c):
                act.wait_ge(gate_mm, u + 1)
                wait(act, hu_ready, u - 3)
                act.activation(silu_g[c][:, :], ring(u, c, 0), ACT.Silu).then_inc(silu_ready, 1)

            def split_high(u, c):
                act.wait_ge(he_ready, u + 1)
                wait(act, down_mm, u - 3)
                act.copy(h_hi[c][:, :], h_e[c][:, :]).then_inc(hhi_ready, 1)

            for p, par, _ in pairs(act):
                first = isinstance(p, int) and p == 0
                for c in range(NCH):
                    u = p * NCH + c
                    silu(u, c)
                    if not (first and c == 0):
                        split_high(u - 1, (c - 1) % 4)
                    if isinstance(u, int) and u == 1:
                        copy_h2t(B - 1)
                        h2_high(B - 1)
                    if isinstance(u, int) and u == 2:
                        logit_exp(B - 1)
                    if isinstance(u, int) and u == 6:
                        for k in range(2):
                            copy_combt(B - 2 + k, ps[:, 7, k * SEQ:(k + 1) * SEQ])
                            comb_high(B - 2 + k)
            for c in range(NCH):
                if c == 1:
                    split_high(NPAIR * NCH - 1, 3)
                act.wait_ge(down_mm, (NPAIR - 1) * NCH + c + 1)
                wait(act, y_mm, c - 1)
                act.copy(y_t[c % 2][:, :], acc[c]).then_inc(yt_ready, 1)

        @block.gpsimd
        def _(pool):
            pool.memset(minus_half[:, :], -0.5).then_inc(half_ready, 1)
            pool.memset(unused_pool[:, :], 0.0).then_inc(x2_ready, 1)
            for i in range(2):
                pool.memset(scores_of[i][:, :, E:E + 8], FILLER).then_inc(filler_ready, 1)
            pool.memset(grp[:, :, G:2 * G], FILLER).then_inc(filler_ready, 1)
            pool.wait_ge(half_ready, 1)

            def inverse_root(rs, k0, done, tiles=4):
                pool.wait_ge(rs[0], done + 1)
                at = slice(k0, k0 + tiles)
                pool.tensor_tensor(rstd[:, at], var_eps[:, at], minus_half[:, 0:tiles], ALU.pow
                                   ).then_inc(rs[1], 1)

            def up_low(piece):
                at = (slice(None), piece // 2, slice((piece % 2) * CH, (piece % 2 + 1) * CH))
                pool.tensor_tensor(w_up_lo[at], w_up[at], w_up_hi[at], ALU.subtract
                                   ).then_inc(w_up_split, 1)

            def rotate(n, b, j):
                pool.wait_ge(swap_ready, n + 1)
                sw = swapped[j % 2][:, :].rearrange("p (a t) -> p a t", a=2)
                pool.tensor_tensor(sw, sw, bcast(rope[:, 1, :], 1, 2), ALU.mult).then_inc(sin_done, 1)
                pool.wait_ge(scaled_ready, n + 1)
                pool.wait_ge(sin_done, n + 1)
                wait(pool, s_mm, 2 * (n - 3))
                pool.tensor_tensor(qk[j % 4][:, :], scaled[j % 2][:, :], swapped[j % 2][:, :], ALU.add
                                   ).then_inc(qk_ready, 1)

            inverse_root(rs_a, 0, 0)
            inverse_root(rs_b, 4, 0)
            for c in range(1, NCH):
                inverse_root(rs_a, 0, c)
                if c == 1:
                    pool.wait_ge(w_up_split_hi, 1)
                    up_low(0)
                up_low(c)
                inverse_root(rs_b, 4, c)
            pool.wait_ge(in_s["rope"], 16)
            for n in range(3):
                rotate(n, 0, n)

            def normalise(n, b, j):
                pool.wait_ge(inv_ready, n + 1)
                pool.tensor_tensor(probs[j % 2][:, 2:4, :], probs[j % 2][:, 2:4, :],
                                   inv_sum[j % 2][:, 2:4].unsqueeze(2).to_broadcast([P, 2, SEQ]), ALU.mult
                                   ).then_inc(probs1_ready, 1)

            def residual(b):
                pool.wait_ge(gate_ready, 1)
                pool.wait_ge(fin_copied, b + 1)
                pool.tensor_tensor(att_y[:, :, :], att_y[:, :, :],
                                   mod[:, ds(b, 1), 2, :].to_broadcast([P, 2, D]), ALU.mult
                                   ).then_inc(gated, 1)
                pool.wait_ge(gated, b + 1)
                pool.tensor_tensor(x_sb[:, ds(b * 2, 2), :], att_y[:, :, :], x_sb[:, ds(b * 2, 2), :],
                                   ALU.add).then_inc(x2_ready, 1)

            def h2_low(b):
                pool.wait_ge(h2hi_ready, b + 1)
                cols = ds(b * SEQ, SEQ)
                pool.tensor_tensor(h2_lo[:, cols], h2t_now[:, :], h2_hi[:, cols], ALU.subtract
                                   ).then_inc(h2lo_ready, 1)

            def weights_low(p, par, cols, split):
                pool.wait_ge(w_rounded, p + 1)
                pool.tensor_tensor(w_lo[par][:, cols], w_raw[par][:, cols], w_hi[par][:, cols],
                                   ALU.subtract).then_inc(split, 1)

            gate_up, down_cols = slice(0, 256), slice(256, WVAL)

            normalise(0, 0, 0)
            for n, b, j in steps(pool):
                for stage, by in ((normalise, 1), (rotate, 3)):
                    at = later(b, j, by)
                    if at:
                        stage(n + by, *at)
                if j == NP - 1 and isinstance(b, int) and b == 0:
                    weights_low(0, 0, gate_up, w_split)
                    weights_low(0, 0, down_cols, w_split_down)
                if j == 1 and behind(b, 1):
                    residual(b - 1)
                if j == 3 and behind(b, 1):
                    inverse_root(rs_c, 8, b - 1, 2)
                if j == 0 and behind(b, 2):
                    h2_low(b - 2)
            residual(B - 1)
            h2_low(B - 2)
            inverse_root(rs_c, 8, B - 1, 2)

            def split_low(u, c):
                pool.wait_ge(hhi_ready, u + 1)
                wait(pool, down_mm, u - 3)
                pool.tensor_tensor(h_lo[c][:, :], h_e[c][:, :], h_hi[c][:, :], ALU.subtract
                                   ).then_inc(hlo_ready, 1)

            for p, par, loads in pairs(pool):
                for c in range(NCH):
                    if isinstance(p, int) and p == 0 and c == 1:
                        h2_low(B - 1)
                    if c == 2 and loads is not None:
                        weights_low(p + 1, 1 - par, gate_up, w_split)
                    if c == 3 and loads is not None:
                        weights_low(p + 1, 1 - par, down_cols, w_split_down)
                    split_low(p * NCH + c, c)
            pool.wait_ge(y_gated, 3)
            pool.tensor_tensor(y[2][:, :, :], y[2][:, :, :], x_sb[:, 8:12, :], ALU.add
                               ).then_inc(y_ready_pool, 1)


def rope_tables():
    inv = 1.0 / 10000.0 ** (np.arange(0, DH, 2, dtype=np.float32) / DH)
    f = np.outer(np.arange(SEQ, dtype=np.float32), inv)
    cos = np.concatenate([np.cos(f), np.cos(f)], -1)[:, ::2]
    sin = np.concatenate([np.sin(f), np.sin(f)], -1)[:, ::2]
    feat = np.arange(P) % DH
    sign = np.where(feat % 2 == 0, -1.0, 1.0).astype(np.float32)
    return np.stack([cos[:, feat // 2].T, sin[:, feat // 2].T * sign[:, None]], 1).astype(np.float32)


def kernel(**inputs):
    import concourse.bacc as bacc
    from concourse.bass_utils import run_bass_kernel_spmd as run

    a = {k: np.asarray(v) for k, v in inputs.items()}
    f = {}
    f["x"] = a["L0_attn_x"].reshape(T, D)
    f["c_t"] = a["L0_c"].T
    f["w_mod"] = a["L0_wmod"]
    wd = [a["L0_attn_w_down_q"].T, a["L0_attn_w_down_kv"].T]
    f["w_down"] = np.stack([np.concatenate([w, w], 1) for w in wd], 1)
    wu = [a["L0_attn_w_up_q"].T, a["L0_attn_w_up_k"].T]
    f["w_up"] = np.stack([np.concatenate([w, w], 0) for w in wu], 1)
    wv = a["L0_attn_w_up_v"].reshape(NP, 2, DH, DL)
    diag = np.zeros((P, NP, P), np.float32)
    diag[0:DH, :, 0:DL] = wv[:, 0].transpose(1, 0, 2)
    diag[DH:P, :, DL:P] = wv[:, 1].transpose(1, 0, 2)
    f["wv_diag"] = diag
    f["wo_t"] = a["L0_attn_w_out"].T.reshape(NP, P, D).transpose(1, 0, 2)
    f["ln_col"] = np.stack([a["L0_attn_ln_scale"], a["L0_attn_ln_bias"]], 1)
    f["rope"] = rope_tables()
    f["ident"] = np.eye(P, dtype=np.float32)
    f["gate_w"] = a["L0_ffn_gate_w"].T
    f["gate_b"] = a["L0_ffn_gate_bias"].reshape(1, E)
    w = np.zeros((NPAIR, P, WCOL), np.float32)
    w[0, :, 0:128] = a["L0_ffn_sg_w"].T
    w[0, :, 128:256] = a["L0_ffn_su_w"].T
    w[0, :, 256:384] = a["L0_ffn_sd_w"].T
    w[1:, :, 0:128] = a["L0_ffn_eg_w"].reshape(E // 2, P, D).transpose(0, 2, 1)
    w[1:, :, 128:256] = a["L0_ffn_eu_w"].reshape(E // 2, P, D).transpose(0, 2, 1)
    for e in range(E):
        at = slice(WVAL + INTER * (e % 2), WVAL + INTER * (e % 2 + 1))
        w[1 + e // 2, e, at] = 1.0
        w[1 + e // 2, E + e, at] = 1.0
    w[1:, :, 256:384] = a["L0_ffn_ed_w"].transpose(0, 2, 1).reshape(E // 2, P, D)
    f["w_pairs"] = w

    nc = bacc.Bacc("TRN2", target_bir_lowering=False, num_devices=1)
    arrays, io = {}, {}
    for name, v in f.items():
        v = np.ascontiguousarray(v)
        arrays["in_" + name] = v
        io[name] = nc.dram_tensor("in_" + name, v.shape, F32, kind="ExternalInput").ap()
    out = nc.dram_tensor("out_0", (T, D), F32, kind="ExternalOutput").ap()
    adaln_kernel(nc, io, out)
    r = run(nc, [arrays], core_ids=[0])
    return r.results[0]["out_0"].reshape(B, SEQ, D)
```
